# Optimizing a Trainium2 kernel written in Bass

```python
import numpy as np
import jax
import jax.numpy as jnp

def _softmax(x, axis=-1):
    return jax.nn.softmax(x, axis=axis)

def _gelu(x):
    return jax.nn.gelu(x, approximate=True)

def _silu(x):
    return jax.nn.silu(x)

def _sigmoid(x):
    return jax.nn.sigmoid(x)

def _layernorm(x, axis=-1, eps=1e-05):
    m = jnp.mean(x, axis=axis, keepdims=True)
    v = jnp.var(x, axis=axis, keepdims=True)
    return (x - m) / jnp.sqrt(v + eps)

def _scatter_add(tgt, idx, src, axis=0):
    return tgt.at[idx].add(src)

def _segment_sum(src, seg, n):
    return jax.ops.segment_sum(src, seg, n)
kernel_name = 'mk_macaron_d1_jaxref_r8_de7a00'

def setup_inputs(seed: int=0):
    np.random.seed(seed)
    _w = jnp.asarray

    def _L0_attn_setup():
        import jax, jax.numpy as jnp
        import numpy as np
        B, S, E, H = (2, 256, 128, 16)
        HD = E // H

        def _rope_tables(seq_len, head_dim, dtype=jnp.float32):
            i = jnp.arange(head_dim // 2, dtype=dtype)
            angles = jnp.power(jnp.asarray(10000.0, dtype), 2.0 * i / head_dim)
            theta = jnp.arange(seq_len, dtype=dtype)[:, None] * angles[None, :]
            cos = jnp.cos(theta)[None, :, None, :]
            sin = jnp.sin(theta)[None, :, None, :]
            return (cos, sin)

        def _apply_rope(t, cos, sin):
            tr, ti = (t[..., 0::2], t[..., 1::2])
            out_r = tr * cos - ti * sin
            out_i = tr * sin + ti * cos
            return jnp.stack([out_r, out_i], axis=-1).reshape(t.shape)
        key = jax.random.key(seed)
        ks = jax.random.split(key, 5)
        x = jax.random.normal(ks[0], (B, S, E), dtype=jnp.float32)
        w_q = jax.random.normal(ks[1], (H * HD, E), dtype=jnp.float32) * 0.02
        w_k = jax.random.normal(ks[2], (H * HD, E), dtype=jnp.float32) * 0.02
        w_v = jax.random.normal(ks[3], (H * HD, E), dtype=jnp.float32) * 0.02
        w_o = jax.random.normal(ks[4], (E, H * HD), dtype=jnp.float32) * 0.02
        return {'x': x, 'w_q': w_q, 'w_k': w_k, 'w_v': w_v, 'w_o': w_o}
    _L0_attn_in = _L0_attn_setup()

    def _L0_ffn_setup():
        import jax, jax.numpy as jnp
        import numpy as np
        D = 128
        H = 512
        E = 8
        B = 2
        T = 256
        LN_EPS = 1e-05

        def _layer_norm(r, gamma, beta):
            mu = jnp.mean(r, axis=-1, keepdims=True)
            var = jnp.mean(jnp.square(r - mu), axis=-1, keepdims=True)
            return (r - mu) * jax.lax.rsqrt(var + LN_EPS) * gamma + beta
        key = jax.random.key(seed)
        ks = jax.random.split(key, 9)
        s_in = 1.0 / np.sqrt(D)
        s_hid = 1.0 / np.sqrt(H)
        x = jax.random.normal(ks[0], (B, T, D), dtype=jnp.float32)
        Wg = jax.random.uniform(ks[1], (D, E), jnp.float32, -s_in, s_in)
        bg = jax.random.uniform(ks[2], (E,), jnp.float32, -s_in, s_in)
        W1 = jax.random.uniform(ks[3], (E, D, H), jnp.float32, -s_in, s_in)
        b1 = jax.random.uniform(ks[4], (E, H), jnp.float32, -s_in, s_in)
        W2 = jax.random.uniform(ks[5], (E, H, D), jnp.float32, -s_hid, s_hid)
        b2 = jax.random.uniform(ks[6], (E, D), jnp.float32, -s_hid, s_hid)
        gamma = jnp.ones((D,), jnp.float32)
        beta = jnp.zeros((D,), jnp.float32)
        return {'x': x, 'Wg': Wg, 'bg': bg, 'W1': W1, 'b1': b1, 'W2': W2, 'b2': b2, 'gamma': gamma, 'beta': beta}
    _L0_ffn_in = _L0_ffn_setup()
    _d = {'L0_attn_x': _L0_attn_in['x'], 'L0_attn_w_q': _L0_attn_in['w_q'], 'L0_attn_w_k': _L0_attn_in['w_k'], 'L0_attn_w_v': _L0_attn_in['w_v'], 'L0_attn_w_o': _L0_attn_in['w_o'], 'L0_ffn_Wg': _L0_ffn_in['Wg'], 'L0_ffn_bg': _L0_ffn_in['bg'], 'L0_ffn_W1': _L0_ffn_in['W1'], 'L0_ffn_b1': _L0_ffn_in['b1'], 'L0_ffn_W2': _L0_ffn_in['W2'], 'L0_ffn_b2': _L0_ffn_in['b2'], 'L0_ffn_gamma': _L0_ffn_in['gamma'], 'L0_ffn_beta': _L0_ffn_in['beta']}
    _x0 = _d['L0_attn_x']
    _d['L0_attn_x'] = jax.random.normal(jax.random.fold_in(jax.random.key(seed), 1), (8, 256, 128), dtype=_x0.dtype)
    del _x0
    return _d

def reference(L0_attn_x, L0_attn_w_q, L0_attn_w_k, L0_attn_w_v, L0_attn_w_o, L0_ffn_Wg, L0_ffn_bg, L0_ffn_W1, L0_ffn_b1, L0_ffn_W2, L0_ffn_b2, L0_ffn_gamma, L0_ffn_beta):

    def _L0_attn_ref(x, w_q, w_k, w_v, w_o):
        import jax, jax.numpy as jnp
        import numpy as np
        B, S, E, H = (2, 256, 128, 16)
        HD = E // H

        def _rope_tables(seq_len, head_dim, dtype=jnp.float32):
            i = jnp.arange(head_dim // 2, dtype=dtype)
            angles = jnp.power(jnp.asarray(10000.0, dtype), 2.0 * i / head_dim)
            theta = jnp.arange(seq_len, dtype=dtype)[:, None] * angles[None, :]
            cos = jnp.cos(theta)[None, :, None, :]
            sin = jnp.sin(theta)[None, :, None, :]
            return (cos, sin)

        def _apply_rope(t, cos, sin):
            tr, ti = (t[..., 0::2], t[..., 1::2])
            out_r = tr * cos - ti * sin
            out_i = tr * sin + ti * cos
            return jnp.stack([out_r, out_i], axis=-1).reshape(t.shape)
        b, s, _ = x.shape
        q = (x @ w_q.T).reshape(b, s, H, HD)
        k = (x @ w_k.T).reshape(b, s, H, HD)
        v = (x @ w_v.T).reshape(b, s, H, HD)
        cos, sin = _rope_tables(s, HD, x.dtype)
        q = _apply_rope(q, cos, sin)
        k = _apply_rope(k, cos, sin)
        att = jnp.einsum('bqhd,bkhd->bhqk', q, k) / jnp.sqrt(jnp.asarray(HD, x.dtype))
        att = jax.nn.softmax(att, axis=-1)
        y = jnp.einsum('bhqk,bkhd->bqhd', att, v).reshape(b, s, H * HD)
        return y @ w_o.T

    def _L0_ffn_ref(x, Wg, bg, W1, b1, W2, b2, gamma, beta):
        import jax, jax.numpy as jnp
        import numpy as np
        D = 128
        H = 512
        E = 8
        B = 2
        T = 256
        LN_EPS = 1e-05

        def _layer_norm(r, gamma, beta):
            mu = jnp.mean(r, axis=-1, keepdims=True)
            var = jnp.mean(jnp.square(r - mu), axis=-1, keepdims=True)
            return (r - mu) * jax.lax.rsqrt(var + LN_EPS) * gamma + beta
        logits = jnp.einsum('btd,de->bte', x, Wg) + bg
        top2_vals, top2_idx = jax.lax.top_k(logits, 2)
        scores = jax.nn.softmax(top2_vals, axis=-1)
        onehot = jax.nn.one_hot(top2_idx, E, dtype=x.dtype)
        combine = jnp.einsum('btk,btke->bte', scores, onehot)
        h = jnp.einsum('btd,edh->bteh', x, W1) + b1[None, None]
        h = jax.nn.gelu(h, approximate=False)
        y = jnp.einsum('bteh,ehd->bted', h, W2) + b2[None, None]
        out = jnp.einsum('bted,bte->btd', y, combine)
        return _layer_norm(x + out, gamma, beta)
    x = L0_attn_x
    x = x + 0.5 * _L0_ffn_ref(_layernorm(x, axis=-1), L0_ffn_Wg, L0_ffn_bg, L0_ffn_W1, L0_ffn_b1, L0_ffn_W2, L0_ffn_b2, L0_ffn_gamma, L0_ffn_beta)
    x = x + _L0_attn_ref(_layernorm(x, axis=-1), L0_attn_w_q, L0_attn_w_k, L0_attn_w_v, L0_attn_w_o)
    x = x + 0.5 * _L0_ffn_ref(_layernorm(x, axis=-1), L0_ffn_Wg, L0_ffn_bg, L0_ffn_W1, L0_ffn_b1, L0_ffn_W2, L0_ffn_b2, L0_ffn_gamma, L0_ffn_beta)
    return x

_drawn_inputs = setup_inputs


def setup_inputs(seed=0):
    import zlib

    import numpy as np

    out = dict(_drawn_inputs(seed))
    spreads = {'L0_ffn_gamma': (1.0, 0.2), 'L0_ffn_beta': (0.0, 0.1)}
    factors = {'L0_attn_w_q': 8.0,
     'L0_attn_w_k': 8.0,
     'L0_attn_w_v': 8.0,
     'L0_attn_w_o': 8.0,
     'L0_ffn_bg': 3.427,
     'L0_ffn_b1': 6.882,
     'L0_ffn_b2': 5.068}
    for name, (base, spread) in spreads.items():
        noise = np.random.default_rng([zlib.crc32(name.encode()), seed]).standard_normal(out[name].shape)
        drawn = base * np.exp(spread * noise) if base else spread * noise
        out[name] = jnp.asarray(drawn.astype(out[name].dtype))
    for name, factor in factors.items():
        out[name] = (out[name] * factor).astype(out[name].dtype)
    return out
```

```python
from contextlib import ExitStack

import concourse.bass as bass
import numpy as np
from concourse import mybir

F32 = mybir.dt.float32
F32R = mybir.dt.float32r
U32 = mybir.dt.uint32
ALU = mybir.AluOpType
ACT = mybir.ActivationFunctionType
AX = mybir.AxisListType

P = 128
BATCH, SEQ, D = 8, 256, 128
HEADS, HD = 16, 8
EXPERTS, HID = 8, 512
LN_EPS = 1e-5
TOKENS = BATCH * SEQ
TILES = TOKENS // P
GROUP = 512
GROUPS = TOKENS // GROUP
GT = GROUP // P
CH = HID // P
STEPS = GROUPS * EXPERTS
BT = SEQ // P
HG = 4
SLOT = P // HG
TU = 16
SU = 8
SCALE = HD ** -0.5
SMALL = 9
M0, M1 = 6, 7


class Steps:

    def __init__(self, base):
        self.base, self.n = base, 0

    def up(self):
        self.n += 1
        return 1

    def now(self):
        return self.base + self.n


V_NORM, V_GATE, V_TAIL = GT, 8, GT + 2
V_ANORM, V_ROPE, V_DIVIDE = BT, 2, BT
V_ATT = V_ANORM + V_ROPE + V_DIVIDE


def build(nc, x, w1, w2, wg, bg, b1, b2, gamma, beta, watt, rope, sel, ones_at, eye, iota8, out):
    with ExitStack() as ctx:
        def sb(name, shape, dt=F32):
            return ctx.enter_context(nc.sbuf_tensor(name, shape, dt))

        def sem(name):
            return ctx.enter_context(nc.semaphore(name))

        ps = ctx.enter_context(nc.psum_tensor("ps", [P, 8, 512], F32))
        gate_rows = nc.dram_tensor("gate_rows", [2 * GROUPS, EXPERTS, GROUP], F32, kind="Internal").ap()

        x_tok = sb("x_tok", [P, TILES, D])
        w_hi = sb("w_hi", [P, 2, EXPERTS, HID], F32R)
        w_lo = sb("w_lo", [P, 2, EXPERTS, HID], F32R)
        x_hi = sb("x_hi", [P, TOKENS], F32R)
        x_lo = sb("x_lo", [P, TOKENS], F32R)
        ident = sb("ident", [P, P])
        ident_r = sb("ident_r", [P, P], F32R)
        wg_sb = sb("wg_sb", [P, EXPERTS])
        bg_sb = sb("bg_sb", [P, EXPERTS])
        b1_sb = sb("b1_sb", [P, EXPERTS, CH])
        b2_sb = sb("b2_sb", [EXPERTS, D])
        gam = sb("gam", [P, D])
        bet = sb("bet", [P, D])
        iota_sb = sb("iota_sb", [P, EXPERTS])
        wa_hi = sb("wa_hi", [P, 6, P], F32R)
        wa_lo = sb("wa_lo", [P, 6, P], F32R)
        sel_r = sb("sel_r", [P, 4, HG, P], F32R)
        rope_sb = sb("rope_sb", [P, 2, SEQ])
        shift_row = sb("shift_row", [P, 1])
        small = sb("small", [P, 8, GT])
        neg_half, euler, eps = small[:, 0, :], small[:, 1, :], small[:, 2, :]
        pad = small[:, 3, 0:1]
        rstd, gap, e2, share1 = small[:, 4, :], small[:, 5, :], small[:, 6, :], small[:, 7, :]

        xn = sb("xn", [P, GT, D])
        post = sb("post", [P, GT, D])
        stats = sb("stats", [P, GT, 6])
        mv = sb("mv", [P, GT, 2])
        logits = sb("logits", [P, GT, EXPERTS])
        top = sb("top", [P, GT, 8])
        top_at = sb("top_at", [P, GT, 8], U32)
        top_f = sb("top_f", [P, GT, 2])
        share2 = sb("share2", [P, GT])
        pick1 = sb("pick1", [P, GT, EXPERTS])
        gates = sb("gates", [P, GT, EXPERTS])
        gates_t = sb("gates_t", [EXPERTS, GROUP])
        mx = pick1[:, :, :].rearrange("p (t a) e -> p t (a e)", t=BT)
        rden = sb("rden", [P, HEADS])

        stage = sb("stage", [P, 2 * EXPERTS * HID])
        ring_hi = sb("ring_hi", [P, 2 * CH * GROUP], F32R)
        ring_lo = sb("ring_lo", [P, 2 * CH * GROUP], F32R)
        ring_g = sb("ring_g", [P, CH * GROUP])
        bcast = sb("bcast", [P, EXPERTS * GROUP])
        acc = sb("acc", [P, GROUP])
        tmp = sb("tmp", [P, 2, GROUP])
        x_t = post[:, :, :].rearrange("p t d -> p (t d)")

        w_raw = stage[:, :].rearrange("p (a e n) -> p a e n", a=2, e=EXPERTS)
        g_hi = ring_hi[:, :].rearrange("p (s c n) -> p s c n", s=2, c=CH)
        g_lo = ring_lo[:, :].rearrange("p (s c n) -> p s c n", s=2, c=CH)
        g_full = ring_g[:, :].rearrange("p (c n) -> p c n", c=CH)
        gate_b = bcast[:, :].rearrange("p (e n) -> p e n", e=EXPERTS)

        sel_raw = stage[:, 0:4 * HG * P]
        wa_raw = stage[:, 4 * HG * P:4 * HG * P + 6 * P]
        prob = stage[:, :].rearrange("p (u n) -> p u n", u=TU)
        qk4 = ring_hi[:, :].rearrange("p (s g m n) -> p s g m n", s=2, g=HG, m=2)
        rot_hi = ring_lo[:, 0:512].rearrange("p (m n) -> p m n", m=2)
        rot_lo = ring_lo[:, 512:1024].rearrange("p (m n) -> p m n", m=2)
        qs4 = ring_lo[:, 1024:2048].rearrange("p (g n) -> p g n", g=HG)
        shift = ring_lo[:, 2048:3072]
        shift_v = shift.rearrange("p (t h c) -> p t h c", t=BT, h=HEADS)
        yt_hi = ring_lo[:, 3072:3328]
        yt_lo = ring_lo[:, 3328:3584]
        t_cos = bcast[:, 0:512].rearrange("p (m n) -> p m n", m=2)
        t_sin = bcast[:, 512:1024].rearrange("p (m n) -> p m n", m=2)
        rot = bcast[:, 1024:1536].rearrange("p (m n) -> p m n", m=2)
        y4 = bcast[:, 1536:2560].rearrange("p (g n) -> p g n", g=HG)
        y_tok = bcast[:, 2560:2816].rearrange("p (t n) -> p t n", t=BT)
        v4 = ring_g[:, :].rearrange("p (s t h c) -> p s t h c", s=2, t=BT, h=HEADS)

        x_loaded = [sem(f"x_loaded{g}") for g in range(GROUPS)]
        w_loaded = [sem(f"w_loaded{e}") for e in range(EXPERTS)]
        eye_loaded, small_loaded, att_loaded = sem("eye_loaded"), sem("small_loaded"), sem("att_loaded")
        consts_set, halved, eye_split = sem("consts_set"), sem("halved"), sem("eye_split")
        w_hi_done, w_split = sem("w_hi_done"), sem("w_split")
        var_ready, rstd_ready = sem("var_ready"), sem("rstd_ready")
        vec_steps = sem("vec_steps")
        ln_done, xt_filled, xt_copied, xlo_done = sem("ln_done"), sem("xt_filled"), sem("xt_copied"), sem("xlo_done")
        logits_filled, gap_ready, e2_ready, gates_ready = (
            sem("logits_filled"), sem("gap_ready"), sem("e2_ready"), sem("gates_ready"))
        gt_filled, gt_copied, gt_stored, base_filled = (
            sem("gt_filled"), sem("gt_copied"), sem("gt_stored"), sem("base_filled"))
        gate_b_loaded = [sem(f"gate_b_loaded{e}") for e in range(EXPERTS)]
        tail_filled, beta_added, x_done = sem("tail_filled"), sem("beta_added"), sem("x_done")
        up_filled, gelu_done, lo_done = sem("up_filled"), sem("gelu_done"), sem("lo_done")
        down_filled, scaled, acc_done = sem("down_filled"), sem("scaled"), sem("acc_done")
        att_split, shift_zeroed, ones_set = sem("att_split"), sem("shift_zeroed"), sem("ones_set")
        a_ln_done, a_xt_filled, a_xhi_done, a_xlo_done = (
            sem("a_ln_done"), sem("a_xt_filled"), sem("a_xhi_done"), sem("a_xlo_done"))
        qk_filled, cos_done, qks_filled, sin_done, rot_ready = (
            sem("qk_filled"), sem("cos_done"), sem("qks_filled"), sem("sin_done"), sem("rot_ready"))
        v_filled, v_ready, sel_filled, qk4_ready = sem("v_filled"), sem("v_ready"), sem("sel_filled"), sem("qk4_ready")
        s_filled, max_done, shift_ready = sem("s_filled"), sem("max_done"), sem("shift_ready")
        qs_filled, qs_ready = sem("qs_filled"), sem("qs_ready")
        t_filled, exp_done = sem("t_filled"), sem("exp_done")
        pv_filled, y4_ready, yq_filled, y_ready = sem("pv_filled"), sem("y4_ready"), sem("yq_filled"), sem("y_ready")
        yt_filled, ythi_done, yt_ready, o_filled, att_done = (
            sem("yt_filled"), sem("ythi_done"), sem("yt_ready"), sem("o_filled"), sem("att_done"))
        stored = sem("stored")

        block = ctx.enter_context(nc.Block())

        LN_FFN = 2 * GROUPS
        LN_ATT = BATCH

        def pre_index(phase, g):
            if isinstance(g, int) and g == 0:
                return phase * (LN_FFN + LN_ATT)
            return phase * (LN_FFN + LN_ATT) + 2 * g - 1

        def post_index(phase, g):
            if isinstance(g, int) and g == GROUPS - 1:
                return phase * (LN_FFN + LN_ATT) + 2 * g + 1
            return phase * (LN_FFN + LN_ATT) + 2 * g + 2

        V_FFN = GROUPS * (V_NORM + V_GATE + V_TAIL)

        def pre_base(phase, g):
            base = phase * (V_FFN + BATCH * V_ATT)
            if isinstance(g, int) and g == 0:
                return base
            return base + g * (V_NORM + V_GATE) + (g - 1) * V_TAIL

        def gate_base(phase, g):
            return pre_base(phase, g) + V_NORM

        def tail_base(phase, g):
            base = phase * (V_FFN + BATCH * V_ATT)
            if isinstance(g, int) and g == GROUPS - 1:
                return base + GROUPS * (V_NORM + V_GATE) + g * V_TAIL
            return base + (g + 2) * (V_NORM + V_GATE) + g * V_TAIL

        def att_base(b):
            if isinstance(b, int) and b == 0:
                return V_FFN
            return V_FFN + b * V_ATT - V_DIVIDE

        def divide_base(b):
            ahead = 1 if isinstance(b, int) and b == BATCH - 1 else 2
            return V_FFN + (b + ahead) * (V_ANORM + V_ROPE) + b * V_DIVIDE

        def tiles(g, n=GT):
            return bass.ds(g * n, n)

        @block.sync
        def _(sp):
            def store_gates(n):
                sp.wait_ge(gt_copied, n + 1)
                sp.dma_start(gate_rows[bass.ds(n, 1), :, :].rearrange("a e n -> (a e) n"),
                             gates_t[:, :]).then_inc(gt_stored, 16)
                sp.wait_ge(gt_stored, 16 * n + 16)

            def load_gates(n, e):
                sp.dma_start(gate_b[:, e, :],
                             gate_rows[bass.ds(n, 1), e, :].broadcast_to([P, GROUP])).then_inc(gate_b_loaded[e], 16)

            def store_x(g):
                sp.wait_ge(x_done, GROUPS + g + 1)
                sp.dma_start(out[tiles(g), :, :].rearrange("t p d -> p t d"),
                             x_tok[:, tiles(g), :]).then_inc(stored, 16)

            def next_gates(phase, g):
                n = phase * GROUPS + g
                store_gates(n + 1)
                for e in range(EXPERTS):
                    sp.wait_ge(scaled, n * EXPERTS + e + 1)
                    load_gates(n + 1, e)

            sp.dma_start(x_tok[:, 0:GT, :], x[0:GT, :, :].rearrange("t p d -> p t d")).then_inc(x_loaded[0], 16)
            sp.dma_start(ident[:, :], eye).then_inc(eye_loaded, 16)
            for e in range(EXPERTS):
                sp.dma_start(w_raw[:, 0, e, :], w1[:, e, :]).then_inc(w_loaded[e], 16)
                sp.dma_start(w_raw[:, 1, e, :], w2[:, e, :]).then_inc(w_loaded[e], 16)
                if e in (1, 3, 5):
                    g = e // 2 + 1
                    sp.dma_start(x_tok[:, g * GT:(g + 1) * GT, :],
                                 x[g * GT:(g + 1) * GT, :, :].rearrange("t p d -> p t d")).then_inc(x_loaded[g], 16)
                if e == 0:
                    for dst, src in ((wg_sb[:, :], wg), (bg_sb[:, :], bg), (b1_sb[:, :, :], b1), (b2_sb[:, :], b2),
                                     (gam[:, :], gamma), (bet[:, :], beta), (iota_sb[:, :], iota8),
                                     (rope_sb[:, :, :], rope), (shift_row[:, :], ones_at)):
                        sp.dma_start(dst, src).then_inc(small_loaded, 16)
            for phase in range(2):
                store_gates(phase * GROUPS)
                for e in range(EXPERTS):
                    if phase:
                        sp.wait_ge(att_done, BATCH)
                    load_gates(phase * GROUPS, e)
                if phase == 0:
                    next_gates(0, 0)
                    sp.wait_ge(w_split, EXPERTS)
                    sp.dma_start(sel_raw, sel).then_inc(att_loaded, 16)
                    sp.dma_start(wa_raw, watt).then_inc(att_loaded, 16)
                    with sp.Fori(1, GROUPS - 1) as g:
                        next_gates(0, g)
                else:
                    with sp.Fori(0, GROUPS - 1) as g:
                        next_gates(1, g)
                        store_x(g)
                    store_x(GROUPS - 1)
            sp.wait_ge(stored, 16 * GROUPS)

        @block.gpsimd
        def _(gp):
            def rstd_of(i, n):
                gp.wait_ge(var_ready, i + 1)
                gp.tensor_tensor(rstd[:, 0:n], mv[:, 0:n, 1], eps[:, 0:n], ALU.add).then_inc(rstd_ready, 1)
                gp.wait_ge(rstd_ready, 2 * i + 1)
                gp.tensor_tensor(rstd[:, 0:n], rstd[:, 0:n], neg_half[:, 0:n], ALU.pow).then_inc(rstd_ready, 1)

            def gate_exp(n):
                gp.wait_ge(gap_ready, n + 1)
                gp.tensor_tensor(e2[:, :], euler[:, :], gap[:, :], ALU.pow).then_inc(e2_ready, 1)

            def split_low(e):
                gp.wait_ge(w_hi_done, e + 1)
                gp.tensor_tensor(w_lo[:, :, e, :], w_raw[:, :, e, :], w_hi[:, :, e, :].bitcast(F32),
                                 ALU.subtract).then_inc(w_split, 1)

            def add_beta(n, g):
                gp.wait_ge(ln_done, n + 1)
                gp.tensor_tensor(x_tok[:, tiles(g), :], x_tok[:, tiles(g), :],
                                 bet[:, :].unsqueeze(1).broadcast_to([P, GT, D]), ALU.add).then_inc(beta_added, 1)

            def body(phase, g, first=False, last=False):
                n = phase * GROUPS + g
                if not last:
                    rstd_of(pre_index(phase, g + 1), GT)
                add_beta(n, g)
                for e in range(1, EXPERTS):
                    gp.wait_ge(scaled, n * EXPERTS + e + 1)
                    gp.wait_ge(acc_done, n * EXPERTS + e)
                    gp.tensor_tensor(acc[:, :], acc[:, :], tmp[:, e % 2, :], ALU.add).then_inc(acc_done, 1)
                    if first and e + 2 < EXPERTS:
                        split_low(e + 2)
                    if e == 3 and not last:
                        gate_exp(n + 1)
                rstd_of(post_index(phase, g), GT)

            gp.memset(neg_half[:, :], -0.5).then_inc(consts_set, 1)
            gp.memset(euler[:, :], float(np.exp(1.0))).then_inc(consts_set, 1)
            gp.memset(eps[:, :], LN_EPS).then_inc(consts_set, 1)
            gp.wait_ge(consts_set, 3)
            gp.wait_ge(small_loaded, 16 * SMALL)
            gp.tensor_scalar(bet[:, :], bet[:, :], 0.5, None, ALU.mult).then_inc(halved, 1)
            gp.tensor_scalar(gam[:, :], gam[:, :], 0.5, None, ALU.mult).then_inc(halved, 1)
            gp.wait_ge(halved, 2)
            rstd_of(pre_index(0, 0), GT)
            split_low(0)
            gate_exp(0)
            split_low(1)
            split_low(2)
            body(0, 0, first=True)
            with gp.Fori(1, GROUPS - 1) as g:
                body(0, g)
            body(0, GROUPS - 1, last=True)

            with gp.Fori(0, BATCH) as b:
                rstd_of(LN_FFN + b, BT)

            rstd_of(pre_index(1, 0), GT)
            gate_exp(GROUPS)
            with gp.Fori(0, GROUPS - 1) as g:
                body(1, g)
            body(1, GROUPS - 1, last=True)

        @block.tensor
        def _(pe):
            def pass3(out_ap, wh, wl, vh, vl, start=True, stop=True):
                pe.matmul(out_ap, wh, vh, start=start, stop=False)
                pe.matmul(out_ap, wh, vl, start=False, stop=False)
                return pe.matmul(out_ap, wl, vh, start=False, stop=stop)

            def transpose_x(n):
                pe.wait_ge(ln_done, n + 1)
                for t in range(GT):
                    mm = pe.transpose(ps[:, M0, t * P:(t + 1) * P], xn[:, t, :], ident[:, :])
                mm.then_inc(xt_filled, 1)

            def router(n):
                pe.wait_ge(xt_copied, n + 1)
                for t in range(GT):
                    mm = pe.matmul(ps[:, M1, t * EXPERTS:(t + 1) * EXPERTS], x_t[:, t * P:(t + 1) * P],
                                   wg_sb[:, :], start=True, stop=True)
                mm.then_inc(logits_filled, 1)

            def transpose_gates(n):
                pe.wait_ge(gates_ready, n + 1)
                for t in range(GT):
                    mm = pe.transpose(ps[0:EXPERTS, M1, t * P:(t + 1) * P], gates[:, t, :], ident[:, :])
                mm.then_inc(gt_filled, 1)

            def base(n, g):
                pe.wait_ge(gt_copied, n + 1)
                cols = bass.ds(g * GROUP, GROUP)
                pe.matmul(ps[:, M0, :], b2_sb[:, :], gates_t[:, :], start=True, stop=False)
                pe.matmul(ps[:, M0, :], ident_r[:, :], x_hi[:, cols], start=False, stop=False)
                pe.matmul(ps[:, M0, :], ident_r[:, :], x_lo[:, cols], start=False, stop=True).then_inc(base_filled, 1)

            def up(n, g, e, split=False):
                if split:
                    pe.wait_ge(w_split, e + 1)
                if e == 0:
                    pe.wait_ge(xlo_done, n + 1)
                s = n * EXPERTS + e
                cols = bass.ds(g * GROUP, GROUP)
                for c in range(CH):
                    if not (isinstance(s, int) and s == 0):
                        pe.wait_ge(gelu_done, (s - 1) * CH + c + 1)
                    w = slice(c * P, (c + 1) * P)
                    pass3(ps[:, c, :], w_hi[:, 0, e, w], w_lo[:, 0, e, w], x_hi[:, cols], x_lo[:, cols])\
                        .then_inc(up_filled, 1)

            def down(n, e):
                s = n * EXPERTS + e
                if not (isinstance(s, int) and s < 2):
                    pe.wait_ge(scaled, s - 1)
                for c in range(CH):
                    pe.wait_ge(lo_done, s * CH + c + 1)
                    w = slice(c * P, (c + 1) * P)
                    mm = pass3(ps[:, 4 + e % 2, :], w_hi[:, 1, e, w], w_lo[:, 1, e, w],
                               g_hi[:, e % 2, c, :], g_lo[:, e % 2, c, :], c == 0, c == CH - 1)
                mm.then_inc(down_filled, 1)

            def transpose_out(n):
                pe.wait_ge(acc_done, EXPERTS * (n + 1))
                for t in range(GT):
                    mm = pe.transpose(ps[:, M1, t * P:(t + 1) * P], acc[:, t * P:(t + 1) * P], ident[:, :])
                mm.then_inc(tail_filled, 1)

            def body(phase, g, first=False, last=False):
                n = phase * GROUPS + g
                for e in range(EXPERTS):
                    down(n, e)
                    if e + 2 < EXPERTS:
                        up(n, g, e + 2, first)
                    elif not last:
                        up(n + 1, g + 1, e + 2 - EXPERTS)
                    if not last:
                        if e == 1:
                            transpose_x(n + 1)
                        if e == 2:
                            router(n + 1)
                        if e == 4:
                            transpose_gates(n + 1)
                        if e == 5:
                            base(n + 1, g + 1)
                transpose_out(n)

            def head(phase):
                n = phase * GROUPS
                transpose_x(n)
                if phase == 0:
                    pe.wait_ge(small_loaded, 16 * SMALL)
                router(n)
                up(n, 0, 0, phase == 0)
                transpose_gates(n)
                base(n, 0)
                up(n, 0, 1, phase == 0)

            def a_transpose_x(b):
                pe.wait_ge(a_ln_done, b + 1)
                for t in range(BT):
                    mm = pe.transpose(ps[:, M0, t * P:(t + 1) * P], xn[:, t, :], ident[:, :])
                mm.then_inc(a_xt_filled, 1)

            def project(b, first_w):
                cols = slice(0, SEQ)
                for m in range(2):
                    mm = pass3(ps[:, M0, m * SEQ:(m + 1) * SEQ], wa_hi[:, first_w + m, :], wa_lo[:, first_w + m, :],
                               x_hi[:, cols], x_lo[:, cols])
                return mm

            def qk(b):
                pe.wait_ge(a_xlo_done, b + 1)
                project(b, 0).then_inc(qk_filled, 1)

            def qk_swapped(b):
                pe.wait_ge(cos_done, b + 1)
                project(b, 2).then_inc(qks_filled, 1)

            def values(b):
                pe.wait_ge(sin_done, b + 1)
                for t in range(BT):
                    cols = slice(t * P, (t + 1) * P)
                    mm = pass3(ps[:, M0, t * P:(t + 1) * P], x_hi[:, cols], x_lo[:, cols],
                               wa_hi[:, 4, :], wa_lo[:, 4, :])
                mm.then_inc(v_filled, 1)

            def place(b, g):
                if g == 0:
                    pe.wait_ge(rot_ready, b + 1)
                    pe.wait_ge(v_ready, b + 1)
                else:
                    pe.wait_ge(qk4_ready, 4 * b + g)
                for m in range(2):
                    o = ps[:, M0, m * SEQ:(m + 1) * SEQ]
                    pe.matmul(o, sel_r[:, 2 * m, g, :], rot_hi[:, m, :], start=True, stop=False)
                    mm = pe.matmul(o, sel_r[:, 2 * m + 1, g, :], rot_lo[:, m, :], start=False, stop=True)
                mm.then_inc(sel_filled, 1)

            def scores(b, p, u):
                pair, t, jp = u // 4, u // 2 % 2, u % 2
                pe.wait_ge(max_done, SU * b + u + 1)
                if u % 4 == 0:
                    pe.wait_ge(qk4_ready, 4 * b + 2 * pair + 2)
                for gg in range(2):
                    for jj in range(2):
                        r = slice(32 * (2 * jp + jj), 32 * (2 * jp + jj) + 32)
                        mm = pe.matmul(ps[:, 2 * (u % 2) + jj, gg * SEQ:(gg + 1) * SEQ],
                                       qk4[r, p, 2 * pair + gg, 0, t * P:(t + 1) * P],
                                       qk4[r, p, 2 * pair + gg, 1, :], start=True, stop=True)
                mm.then_inc(s_filled, 1)

            def place_shifted(b, pair):
                pe.wait_ge(shift_ready, 2 * b + pair + 1)
                for gg in range(2):
                    g = 2 * pair + gg
                    pe.matmul(ps[:, M1, gg * SEQ:(gg + 1) * SEQ], sel_r[:, 0, g, :], rot_hi[:, 0, :],
                              start=True, stop=False, skip_group_check=True)
                    pe.matmul(ps[:, M1, gg * SEQ:(gg + 1) * SEQ], sel_r[:, 1, g, :], rot_lo[:, 0, :],
                              start=False, stop=False, skip_group_check=True)
                    for t in range(BT):
                        mm = pe.matmul(ps[:, M1, gg * SEQ + t * P:gg * SEQ + (t + 1) * P],
                                       shift[:, t * 512 + g * P:t * 512 + (g + 1) * P], ident_r[:, :],
                                       start=False, stop=(t == BT - 1), skip_group_check=True)
                mm.then_inc(qs_filled, 1)

            def scores_t(b, p, u):
                pair, t, j = u // 8, u // 4 % 2, u % 4
                pe.wait_ge(exp_done, TU * b + u + 1)
                if u % 8 == 0:
                    pe.wait_ge(qs_ready, 2 * b + pair + 1)
                r = slice(32 * j, 32 * j + 32)
                for gg in range(2):
                    g = 2 * pair + gg
                    mm = pe.matmul(ps[:, 4 + u % 2, gg * SEQ:(gg + 1) * SEQ],
                                   qk4[r, p, g, 1, t * P:(t + 1) * P], qs4[r, g, :], start=True, stop=True)
                mm.then_inc(t_filled, 1)

            def weigh(b, p, pair):
                pe.wait_ge(exp_done, TU * b + 8 * pair + 8 + 2)
                for gg in range(2):
                    for t in range(BT):
                        for j in range(4):
                            h = 4 * (2 * pair + gg) + j
                            mm = pe.matmul(ps[32 * j:32 * j + 32, M1, gg * SEQ:(gg + 1) * SEQ], v4[:, p, t, h, :],
                                           prob[:, 8 * pair + 4 * t + j, gg * SEQ:(gg + 1) * SEQ],
                                           start=(t == 0), stop=(t == BT - 1))
                mm.then_inc(pv_filled, 1)

            def turn_y(b, t):
                if t == 0:
                    pe.wait_ge(y4_ready, 2 * b + 2)
                else:
                    pe.wait_ge(y_ready, 2 * b + t)
                for g in range(HG):
                    mm = pe.transpose(ps[:, M1, g * P:(g + 1) * P], y4[:, g, t * P:(t + 1) * P], ident[:, :])
                mm.then_inc(yq_filled, 1)

            def transpose_y(b):
                pe.wait_ge(y_ready, 2 * b + 2)
                for t in range(BT):
                    mm = pe.transpose(ps[:, M1, t * P:(t + 1) * P], y_tok[:, t, :], ident[:, :])
                mm.then_inc(yt_filled, 1)

            def project_out(b):
                pe.wait_ge(yt_ready, b + 1)
                for t in range(BT):
                    mm = pass3(ps[:, M1, t * P:(t + 1) * P], yt_hi[:, t * P:(t + 1) * P], yt_lo[:, t * P:(t + 1) * P],
                               wa_hi[:, 5, :], wa_lo[:, 5, :])
                mm.then_inc(o_filled, 1)

            def front(b, p):
                a_transpose_x(b)
                qk(b)
                qk_swapped(b)
                values(b)
                for g in range(HG):
                    place(b, g)
                for u in range(4):
                    scores(b, p, u)
                place_shifted(b, 0)
                for u in range(4, 8):
                    scores(b, p, u)
                pe.wait_ge(qs_ready, 2 * b + 1)
                place_shifted(b, 1)

            def back(b, p, more):
                q = 1 - p

                def t_units(*us):
                    for u in us:
                        scores_t(b, p, u)

                t_units(0, 1)
                if more:
                    a_transpose_x(b + 1)
                t_units(2)
                if more:
                    qk(b + 1)
                t_units(3, 4)
                if more:
                    qk_swapped(b + 1)
                t_units(5)
                if more:
                    values(b + 1)
                t_units(6, 7)
                if more:
                    place(b + 1, 0)
                t_units(8)
                if more:
                    place(b + 1, 1)
                pe.wait_ge(qs_ready, 2 * b + 2)
                weigh(b, p, 0)
                for k in range(4):
                    if more:
                        scores(b + 1, q, k)
                    t_units(9 + k)
                    if more and k in (1, 2):
                        place(b + 1, 1 + k)
                if more:
                    pe.wait_ge(y4_ready, 2 * b + 1)
                    place_shifted(b + 1, 0)
                    scores(b + 1, q, 4)
                t_units(13)
                if more:
                    scores(b + 1, q, 5)
                t_units(14, 15)
                if more:
                    scores(b + 1, q, 6)
                    pe.wait_ge(qs_ready, 2 * b + 3)
                else:
                    pe.wait_ge(y4_ready, 2 * b + 1)
                weigh(b, p, 1)
                if more:
                    scores(b + 1, q, 7)
                turn_y(b, 0)
                turn_y(b, 1)
                transpose_y(b)
                project_out(b)
                if more:
                    pe.wait_ge(att_done, b + 1)
                    place_shifted(b + 1, 1)

            pe.wait_ge(eye_loaded, 16)
            pe.wait_ge(eye_split, 1)
            head(0)
            body(0, 0, first=True)
            with pe.Fori(1, GROUPS - 1) as g:
                body(0, g)
            body(0, GROUPS - 1, last=True)

            pe.wait_ge(att_split, 3)
            pe.wait_ge(shift_zeroed, 1)
            pe.wait_ge(ones_set, 1)
            front(0, 0)
            with pe.Fori(0, BATCH // 2 - 1) as i:
                back(2 * i, 0, True)
                back(2 * i + 1, 1, True)
            back(BATCH - 2, 0, True)
            back(BATCH - 1, 1, False)

            head(1)
            with pe.Fori(0, GROUPS - 1) as g:
                body(1, g)
            body(1, GROUPS - 1, last=True)

        @block.scalar
        def _(act):
            def copy_x(n, g):
                act.wait_ge(xt_filled, n + 1)
                act.activation(x_t[:, :], ps[:, M0, :], ACT.Copy)
                act.activation(x_hi[:, bass.ds(g * GROUP, GROUP)], ps[:, M0, :], ACT.Copy).then_inc(xt_copied, 1)

            def copy_gates(n):
                act.wait_ge(gt_filled, n + 1)
                if not (isinstance(n, int) and n == 0):
                    act.wait_ge(gt_stored, 16 * n)
                act.activation(gates_t[:, :], ps[0:EXPERTS, M1, :], ACT.Copy).then_inc(gt_copied, 1)

            def gelu(n, e):
                s = n * EXPERTS + e
                if not (isinstance(s, int) and s < 2):
                    act.wait_ge(down_filled, s - 1)
                for c in range(CH):
                    act.wait_ge(up_filled, s * CH + c + 1)
                    act.activation(g_hi[:, e % 2, c, :], ps[:, c, :], ACT.Gelu, bias=b1_sb[:, e, c:c + 1])
                    if not (isinstance(s, int) and s == 0):
                        act.wait_ge(lo_done, (s - 1) * CH + c + 1)
                    act.activation(g_full[:, c, :], ps[:, c, :], ACT.Gelu, bias=b1_sb[:, e, c:c + 1])\
                        .then_inc(gelu_done, 1)

            def body(phase, g, last=False):
                n = phase * GROUPS + g
                for e in range(EXPERTS):
                    if e + 2 < EXPERTS:
                        gelu(n, e + 2)
                    elif not last:
                        gelu(n + 1, e + 2 - EXPERTS)
                    if not last:
                        if e == 1:
                            copy_x(n + 1, g + 1)
                        if e == 4:
                            copy_gates(n + 1)

            def head(phase):
                n = phase * GROUPS
                copy_x(n, 0)
                gelu(n, 0)
                copy_gates(n)
                gelu(n, 1)

            def a_copy_x(b):
                act.wait_ge(a_xt_filled, b + 1)
                act.activation(x_hi[:, 0:SEQ], ps[:, M0, 0:SEQ], ACT.Copy).then_inc(a_xhi_done, 1)

            def copy_values(b, p):
                act.wait_ge(v_filled, b + 1)
                act.activation(v4[:, p, :, :, 0:HD],
                               ps[:, M0, 0:SEQ].rearrange("p (t h c) -> p t h c", t=BT, h=HEADS),
                               ACT.Copy).then_inc(v_ready, 1)

            def copy_placed(b, p, g):
                act.wait_ge(sel_filled, 4 * b + g + 1)
                act.activation(qk4[:, p, g, 0, :], ps[:, M0, 0:SEQ], ACT.Copy)
                act.activation(qk4[:, p, g, 1, :], ps[:, M0, SEQ:2 * SEQ], ACT.Identity,
                               bias=shift_row[:, :]).then_inc(qk4_ready, 1)

            def copy_shifted(b, pair):
                act.wait_ge(qs_filled, 2 * b + pair + 1)
                act.activation(qs4[:, 2 * pair:2 * pair + 2, :],
                               ps[:, M1, :].rearrange("p (g n) -> p g n", g=2), ACT.Copy).then_inc(qs_ready, 1)

            def exps(b, *us):
                for u in us:
                    act.wait_ge(t_filled, TU * b + u + 1)
                    act.activation(prob[:, u, :], ps[:, 4 + u % 2, :], ACT.Exp, scale=SCALE).then_inc(exp_done, 1)

            def copy_weighed(b, pair):
                act.wait_ge(pv_filled, 2 * b + pair + 1)
                act.activation(y4[:, 2 * pair:2 * pair + 2, :],
                               ps[:, M1, :].rearrange("p (g n) -> p g n", g=2), ACT.Copy).then_inc(y4_ready, 1)

            def copy_y(b):
                act.wait_ge(yt_filled, b + 1)
                act.activation(yt_hi, ps[:, M1, 0:SEQ], ACT.Copy).then_inc(ythi_done, 1)

            def front(b, p):
                a_copy_x(b)
                copy_values(b, p)
                for g in range(HG):
                    copy_placed(b, p, g)
                copy_shifted(b, 0)
                copy_shifted(b, 1)

            def back(b, p, more):
                q = 1 - p
                exps(b, 0, 1)
                if more:
                    a_copy_x(b + 1)
                exps(b, 2, 3, 4, 5)
                if more:
                    copy_values(b + 1, q)
                exps(b, 6, 7)
                if more:
                    copy_placed(b + 1, q, 0)
                exps(b, 8)
                if more:
                    copy_placed(b + 1, q, 1)
                copy_weighed(b, 0)
                exps(b, 9, 10)
                if more:
                    copy_placed(b + 1, q, 2)
                exps(b, 11)
                if more:
                    copy_placed(b + 1, q, 3)
                exps(b, 12)
                if more:
                    copy_shifted(b + 1, 0)
                exps(b, 13, 14, 15)
                copy_weighed(b, 1)
                copy_y(b)
                if more:
                    copy_shifted(b + 1, 1)

            act.wait_ge(small_loaded, 16 * SMALL)
            head(0)
            with act.Fori(0, GROUPS - 1) as g:
                body(0, g)
            body(0, GROUPS - 1, last=True)

            act.sem_inc(exp_done, 2)
            act.wait_ge(ones_set, 1)
            act.wait_ge(att_split, 3)
            front(0, 0)
            with act.Fori(0, BATCH // 2 - 1) as i:
                back(2 * i, 0, True)
                back(2 * i + 1, 1, True)
            back(BATCH - 2, 0, True)
            back(BATCH - 1, 1, False)

            head(1)
            with act.Fori(0, GROUPS - 1) as g:
                body(1, g)
            body(1, GROUPS - 1, last=True)

        @block.vector
        def _(vec):
            def normalize(dst, src, count, i, base):
                at = Steps(base)
                for t in range(count):
                    vec.bn_stats(stats[:, t, :], src(t)).then_inc(vec_steps, at.up())
                vec.wait_ge(vec_steps, base + count)
                vec.memset(pad[:, :], 0.0)
                for t in range(count):
                    aggr = vec.bn_aggr(mv[:, t, :], stats[:, t, :])
                aggr.then_inc(var_ready, 1)
                vec.wait_ge(var_ready, i + 1)
                vec.wait_ge(rstd_ready, 2 * i + 2)
                for t in range(count):
                    last = vec.tensor_scalar(dst(t), src(t), mv[:, t, 0:1], rstd[:, t:t + 1],
                                             ALU.subtract, ALU.mult)
                return last

            def norm_in(phase, g, n):
                normalize(lambda t: xn[:, t, :], lambda t: x_tok[:, bass.ds(g * GT + t, 1), :].rearrange(
                    "p a d -> p (a d)"), GT, pre_index(phase, g), pre_base(phase, g)).then_inc(ln_done, 1)

            def low_x(n, g):
                vec.wait_ge(xt_copied, n + 1)
                cols = bass.ds(g * GROUP, GROUP)
                vec.tensor_tensor(x_lo[:, cols], ps[:, M0, :], x_hi[:, cols].bitcast(F32),
                                  ALU.subtract).then_inc(xlo_done, 1)

            def gating(phase, g, n):
                at = Steps(gate_base(phase, g))
                vec.wait_ge(logits_filled, n + 1)
                vec.tensor_tensor(logits[:, :, :], ps[:, M1, 0:GT * EXPERTS].rearrange("p (t e) -> p t e", t=GT),
                                  bg_sb[:, :].unsqueeze(1).broadcast_to([P, GT, EXPERTS]),
                                  ALU.add).then_inc(vec_steps, at.up())
                vec.wait_ge(vec_steps, at.now())
                vec.memset(pad[:, :], 0.0)
                for t in range(GT):
                    op = vec.max(top[:, t, :], logits[:, t, :])
                op.then_inc(vec_steps, at.up())
                vec.wait_ge(vec_steps, at.now())
                vec.tensor_tensor(gap[:, :], top[:, :, 1], top[:, :, 0], ALU.subtract).then_inc(gap_ready, 1)
                for t in range(GT):
                    op = vec.max_index(top_at[:, t, :], top[:, t, :], logits[:, t, :])
                op.then_inc(vec_steps, at.up())
                vec.wait_ge(vec_steps, at.now())
                vec.tensor_copy(top_f[:, :, :], top_at[:, :, 0:2]).then_inc(vec_steps, at.up())
                vec.wait_ge(e2_ready, n + 1)
                vec.tensor_scalar(share2[:, :], e2[:, :], 1.0, None, ALU.add).then_inc(vec_steps, at.up())
                vec.wait_ge(vec_steps, at.now())
                vec.reciprocal(share1[:, :], share2[:, :]).then_inc(vec_steps, at.up())
                vec.tensor_tensor(pick1[:, :, :], iota_sb[:, :].unsqueeze(1).broadcast_to([P, GT, EXPERTS]),
                                  top_f[:, :, 0:1].broadcast_to([P, GT, EXPERTS]), ALU.is_equal)
                vec.tensor_tensor(gates[:, :, :], iota_sb[:, :].unsqueeze(1).broadcast_to([P, GT, EXPERTS]),
                                  top_f[:, :, 1:2].broadcast_to([P, GT, EXPERTS]), ALU.is_equal)
                vec.wait_ge(vec_steps, at.now())
                vec.tensor_tensor(share2[:, :], e2[:, :], share1[:, :], ALU.mult).then_inc(vec_steps, at.up())
                vec.wait_ge(vec_steps, at.now())
                vec.tensor_tensor(pick1[:, :, :], pick1[:, :, :],
                                  share1[:, :].unsqueeze(2).broadcast_to([P, GT, EXPERTS]), ALU.mult)
                vec.tensor_tensor(gates[:, :, :], gates[:, :, :],
                                  share2[:, :].unsqueeze(2).broadcast_to([P, GT, EXPERTS]),
                                  ALU.mult).then_inc(vec_steps, at.up())
                vec.wait_ge(vec_steps, at.now())
                vec.tensor_tensor(gates[:, :, :], gates[:, :, :], pick1[:, :, :], ALU.add).then_inc(gates_ready, 1)
                assert at.n == V_GATE

            def scale_out(n, e):
                s = n * EXPERTS + e
                vec.wait_ge(down_filled, s + 1)
                vec.wait_ge(gate_b_loaded[e], 16 * n + 16)
                if not (isinstance(s, int) and s < 2):
                    vec.wait_ge(acc_done, s - 1)
                vec.tensor_tensor(tmp[:, e % 2, :], ps[:, 4 + e % 2, :], gate_b[:, e, :],
                                  ALU.mult).then_inc(scaled, 1)
                if e == 0:
                    vec.wait_ge(scaled, s + 1)
                    vec.wait_ge(base_filled, n + 1)
                    vec.tensor_tensor(acc[:, :], ps[:, M0, :], tmp[:, 0, :], ALU.add).then_inc(acc_done, 1)

            def low_g(n, e):
                s = n * EXPERTS + e
                for c in range(CH):
                    vec.wait_ge(gelu_done, s * CH + c + 1)
                    vec.tensor_tensor(g_lo[:, e % 2, c, :], g_full[:, c, :], g_hi[:, e % 2, c, :].bitcast(F32),
                                      ALU.subtract).then_inc(lo_done, 1)

            def finish(phase, g, n):
                base = tail_base(phase, g)
                vec.wait_ge(tail_filled, n + 1)
                normalize(lambda t: post[:, t, :], lambda t: ps[:, M1, t * P:(t + 1) * P],
                          GT, post_index(phase, g), base).then_inc(vec_steps, 1)
                vec.wait_ge(vec_steps, base + GT + 1)
                vec.tensor_tensor(post[:, :, :], post[:, :, :], gam[:, :].unsqueeze(1).broadcast_to([P, GT, D]),
                                  ALU.mult).then_inc(vec_steps, 1)
                vec.wait_ge(vec_steps, base + GT + 2)
                vec.wait_ge(beta_added, n + 1)
                vec.tensor_tensor(x_tok[:, tiles(g), :], x_tok[:, tiles(g), :], post[:, :, :],
                                  ALU.add).then_inc(x_done, 1)

            def split_high(e):
                vec.wait_ge(w_loaded[e], 32)
                vec.tensor_copy(w_hi[:, :, e, :], w_raw[:, :, e, :]).then_inc(w_hi_done, 1)

            def body(phase, g, first=False, last=False):
                n = phase * GROUPS + g
                for e in range(EXPERTS):
                    scale_out(n, e)
                    if e + 2 < EXPERTS:
                        low_g(n, e + 2)
                    elif not last:
                        low_g(n + 1, e + 2 - EXPERTS)
                    if first and e + 3 < EXPERTS:
                        split_high(e + 3)
                    if not last:
                        if e == 0:
                            if first:
                                for later in x_loaded[1:]:
                                    vec.wait_ge(later, 16)
                            norm_in(phase, g + 1, n + 1)
                        if e == 2:
                            low_x(n + 1, g + 1)
                        if e == 3:
                            gating(phase, g + 1, n + 1)
                finish(phase, g, n)

            def head(phase):
                n = phase * GROUPS
                norm_in(phase, 0, n)
                if phase == 0:
                    split_high(0)
                low_x(n, 0)
                if phase == 0:
                    split_high(1)
                    split_high(2)
                    vec.wait_ge(small_loaded, 16 * SMALL)
                gating(phase, 0, n)
                low_g(n, 0)
                low_g(n, 1)

            def a_norm(b):
                if isinstance(b, int) and b == 0:
                    vec.wait_ge(x_done, GROUPS)
                normalize(lambda t: xn[:, t, :], lambda t: x_tok[:, bass.ds(b * BT + t, 1), :].rearrange(
                    "p a d -> p (a d)"), BT, LN_FFN + b, att_base(b)).then_inc(a_ln_done, 1)

            def a_low_x(b):
                vec.wait_ge(a_xhi_done, b + 1)
                cols = slice(0, SEQ)
                vec.tensor_tensor(x_lo[:, cols], ps[:, M0, 0:SEQ], x_hi[:, cols].bitcast(F32),
                                  ALU.subtract).then_inc(a_xlo_done, 1)

            def rotate_cos(b):
                vec.wait_ge(qk_filled, b + 1)
                vec.tensor_tensor(t_cos, ps[:, M0, :].rearrange("p (m n) -> p m n", m=2),
                                  rope_sb[:, 0:1, :].broadcast_to([P, 2, SEQ]), ALU.mult).then_inc(cos_done, 1)

            def rotate_sin(b):
                at = Steps(att_base(b) + V_ANORM)
                vec.wait_ge(qks_filled, b + 1)
                vec.tensor_tensor(t_sin, ps[:, M0, :].rearrange("p (m n) -> p m n", m=2),
                                  rope_sb[:, 1:2, :].broadcast_to([P, 2, SEQ]), ALU.mult).then_inc(sin_done, 1)
                vec.wait_ge(sin_done, b + 1)
                vec.tensor_tensor(rot, t_cos, t_sin, ALU.add).then_inc(vec_steps, at.up())
                vec.wait_ge(vec_steps, at.now())
                vec.tensor_copy(rot_hi, rot).then_inc(vec_steps, at.up())
                vec.wait_ge(vec_steps, at.now())
                vec.tensor_tensor(rot_lo, rot, rot_hi.bitcast(F32), ALU.subtract).then_inc(rot_ready, 1)

            def maxima(b, *us):
                for u in us:
                    pair, t, jp = u // 4, u // 2 % 2, u % 2
                    vec.wait_ge(s_filled, SU * b + u + 1)
                    first = 8 * pair + 2 * jp
                    vec.tensor_reduce(
                        mx[:, t, :].rearrange("p (r g j) -> p r j g", r=2, g=2)[:, pair, 2 * jp:2 * jp + 2, :],
                        ps[:, 2 * (u % 2):2 * (u % 2) + 2, :].rearrange("p j (g n) -> p j g n", g=2),
                        AX.X, ALU.max).then_inc(max_done, 1)

            def negate(b, pair):
                vec.wait_ge(max_done, SU * b + 4 * pair + 4 + 2)
                vec.tensor_scalar(shift_v[:, :, 8 * pair:8 * pair + 8, 24:25].rearrange("p t h c -> p t (h c)"),
                                  mx[:, :, 8 * pair:8 * pair + 8], -1.0, None, ALU.mult).then_inc(shift_ready, 1)

            def divide(b, t):
                at = Steps(divide_base(b) + t)
                vec.wait_ge(yq_filled, 2 * b + t + 1)
                heads = ps[:, M1, :].rearrange("p (h c) -> p h c", h=HEADS)
                vec.reciprocal(rden[:, :], heads[:, :, HD]).then_inc(vec_steps, at.up())
                vec.wait_ge(vec_steps, at.now())
                vec.tensor_tensor(y_tok[:, t, :].rearrange("p (h c) -> p h c", h=HEADS), heads[:, :, 0:HD],
                                  rden[:, :].unsqueeze(2).broadcast_to([P, HEADS, HD]),
                                  ALU.mult).then_inc(y_ready, 1)

            def low_y(b):
                vec.wait_ge(ythi_done, b + 1)
                vec.tensor_tensor(yt_lo, ps[:, M1, 0:SEQ], yt_hi.bitcast(F32), ALU.subtract).then_inc(yt_ready, 1)

            def add_attention(b):
                vec.wait_ge(o_filled, b + 1)
                vec.tensor_tensor(x_tok[:, tiles(b, BT), :], ps[:, M1, 0:SEQ].rearrange("p (t d) -> p t d", t=BT),
                                  x_tok[:, tiles(b, BT), :], ALU.add).then_inc(att_done, 1)

            def front(b):
                a_norm(b)
                a_low_x(b)
                rotate_cos(b)
                rotate_sin(b)
                maxima(b, 0, 1, 2, 3)
                negate(b, 0)
                maxima(b, 4, 5, 6, 7)
                negate(b, 1)

            def back(b, more):
                if more:
                    a_norm(b + 1)
                    a_low_x(b + 1)
                    rotate_cos(b + 1)
                    rotate_sin(b + 1)
                    maxima(b + 1, 0, 1, 2, 3)
                    negate(b + 1, 0)
                    maxima(b + 1, 4, 5, 6, 7)
                    negate(b + 1, 1)
                divide(b, 0)
                divide(b, 1)
                low_y(b)
                add_attention(b)

            vec.wait_ge(eye_loaded, 16)
            vec.tensor_copy(ident_r[:, :], ident[:, :]).then_inc(eye_split, 1)
            vec.wait_ge(x_loaded[0], 16)
            head(0)
            body(0, 0, first=True)
            with vec.Fori(1, GROUPS - 1) as g:
                body(0, g)
            body(0, GROUPS - 1, last=True)

            vec.wait_ge(att_loaded, 32)
            vec.tensor_copy(sel_r[:, :, :, :].rearrange("p a g m -> p (a g m)"), sel_raw).then_inc(att_split, 1)
            vec.tensor_copy(wa_hi[:, :, :].rearrange("p a m -> p (a m)"), wa_raw).then_inc(att_split, 1)
            vec.wait_ge(att_split, 2)
            vec.tensor_tensor(wa_lo[:, :, :].rearrange("p a m -> p (a m)"), wa_raw,
                              wa_hi[:, :, :].rearrange("p a m -> p (a m)").bitcast(F32),
                              ALU.subtract).then_inc(att_split, 1)
            vec.memset(ring_g[:, :], 1.0).then_inc(ones_set, 1)
            vec.memset(shift.bitcast(F32), 0.0).then_inc(shift_zeroed, 1)
            vec.sem_inc(max_done, 2)
            front(0)
            with vec.Fori(0, BATCH - 1) as b:
                back(b, True)
            back(BATCH - 1, False)

            head(1)
            with vec.Fori(0, GROUPS - 1) as g:
                body(1, g)
            body(1, GROUPS - 1, last=True)


def shape_constants():
    pair = np.arange(HD // 2, dtype=np.float32)
    angle = np.power(np.float32(10000.0), np.float32(2.0) * pair / np.float32(HD)).astype(np.float32)
    theta = (np.arange(SEQ, dtype=np.float32)[:, None] * angle[None, :]).astype(np.float32)
    cos, sin = np.cos(theta).astype(np.float32), np.sin(theta).astype(np.float32)
    rope = np.zeros((P, 2, SEQ), np.float32)
    for c in range(P):
        rope[c, 0] = cos[:, c % HD // 2]
        rope[c, 1] = sin[:, c % HD // 2] * (1 if c % 2 else -1)
    sel = np.zeros((P, 4, HG, P), np.float32)
    parts = ((0, 2), (1,), (0, 1), (2,))
    for kind, eights in enumerate(parts):
        for h in range(HEADS):
            g, j = h // 4, h % 4
            for r in eights:
                for c in range(HD):
                    sel[HD * h + c, kind, g, SLOT * j + HD * r + c] = 1.0
    ones_at = np.zeros((P, 1), np.float32)
    ones_at[24::SLOT] = 1.0
    iota8 = np.ascontiguousarray(np.broadcast_to(np.arange(EXPERTS, dtype=np.float32), (P, EXPERTS)))
    return dict(rope=rope, sel=sel.reshape(P, -1), ones_at=ones_at, eye=np.eye(P, dtype=np.float32), iota8=iota8)


def kernel(L0_attn_x, L0_attn_w_q, L0_attn_w_k, L0_attn_w_v, L0_attn_w_o, L0_ffn_Wg, L0_ffn_bg, L0_ffn_W1,
           L0_ffn_b1, L0_ffn_W2, L0_ffn_b2, L0_ffn_gamma, L0_ffn_beta):
    import concourse.bacc as bacc
    from concourse.bass_utils import run_bass_kernel_spmd

    def rows(a):
        a = np.asarray(a)
        return np.ascontiguousarray(np.broadcast_to(a, (P,) + a.shape))

    swap = np.arange(P).reshape(-1, 2)[:, ::-1].reshape(-1)
    wq, wk, wv, wo = (np.asarray(w) for w in (L0_attn_w_q, L0_attn_w_k, L0_attn_w_v, L0_attn_w_o))
    w1, w2 = np.asarray(L0_ffn_W1), np.asarray(L0_ffn_W2)
    arrays = dict(
        x=np.asarray(L0_attn_x).reshape(TILES, P, D),
        w1=w1.transpose(1, 0, 2),
        w2=w2.reshape(EXPERTS, CH, P, D).transpose(2, 0, 1, 3).reshape(P, EXPERTS, HID),
        wg=np.asarray(L0_ffn_Wg),
        bg=rows(L0_ffn_bg),
        b1=np.asarray(L0_ffn_b1).reshape(EXPERTS, CH, P).transpose(2, 0, 1),
        b2=np.asarray(L0_ffn_b2),
        gamma=rows(L0_ffn_gamma),
        beta=rows(L0_ffn_beta),
        watt=np.stack([wq.T, wk.T, wq[swap].T, wk[swap].T, wv.T, wo.T], axis=1).reshape(P, 6 * P),
        **shape_constants(),
    )
    arrays = {n: np.ascontiguousarray(a) for n, a in arrays.items()}
    nc = bacc.Bacc("TRN2", target_bir_lowering=False, num_devices=1)
    args = {n: nc.dram_tensor(n, a.shape, mybir.dt.from_np(a.dtype), kind="ExternalInput").ap()
            for n, a in arrays.items()}
    args["out"] = nc.dram_tensor("out", (TILES, P, D), F32, kind="ExternalOutput").ap()
    build(nc, **args)
    result = run_bass_kernel_spmd(nc, [arrays], core_ids=[0])
    return result.results[0]["out"].reshape(BATCH, SEQ, D)
```

```python
from contextlib import ExitStack

import concourse.bass as bass
import numpy as np
from concourse import mybir

F32 = mybir.dt.float32
F32R = mybir.dt.float32r
U32 = mybir.dt.uint32
ALU = mybir.AluOpType
ACT = mybir.ActivationFunctionType
AX = mybir.AxisListType

P = 128
BATCH, SEQ, D = 8, 256, 128
HEADS, HD = 16, 8
EXPERTS, HID = 8, 512
LN_EPS = 1e-5
TOKENS = BATCH * SEQ
TILES = TOKENS // P
GROUP = 512
GROUPS = TOKENS // GROUP
GT = GROUP // P
CH = HID // P
STEPS = GROUPS * EXPERTS
BT = SEQ // P
HG = 4
SLOT = P // HG
TU = 16
SU = 8
SCALE = HD ** -0.5
SMALL = 9
M0, M1 = 6, 7


class Steps:

    def __init__(self, base):
        self.base, self.n = base, 0

    def up(self):
        self.n += 1
        return 1

    def now(self):
        return self.base + self.n


GATE_STEPS = 8


def build(nc, x, w1, w2, wg, bg, b1, b2, gamma, beta, watt, rope, sel, ones_at, eye, iota8, out):
    with ExitStack() as ctx:
        def sb(name, shape, dt=F32):
            return ctx.enter_context(nc.sbuf_tensor(name, shape, dt))

        def sem(name):
            return ctx.enter_context(nc.semaphore(name))

        ps = ctx.enter_context(nc.psum_tensor("ps", [P, 8, 512], F32))
        gate_rows = nc.dram_tensor("gate_rows", [2 * GROUPS, EXPERTS, GROUP], F32, kind="Internal").ap()

        x_tok = sb("x_tok", [P, TILES, D])
        w_hi = sb("w_hi", [P, 2, EXPERTS, HID], F32R)
        w_lo = sb("w_lo", [P, 2, EXPERTS, HID], F32R)
        x_hi = sb("x_hi", [P, TOKENS], F32R)
        x_lo = sb("x_lo", [P, TOKENS], F32R)
        ident = sb("ident", [P, P])
        ident_r = sb("ident_r", [P, P], F32R)
        wg_sb = sb("wg_sb", [P, EXPERTS])
        bg_sb = sb("bg_sb", [P, EXPERTS])
        b1_sb = sb("b1_sb", [P, EXPERTS, CH])
        b2_sb = sb("b2_sb", [EXPERTS, D])
        gam = sb("gam", [P, D])
        bet = sb("bet", [P, D])
        iota_sb = sb("iota_sb", [P, EXPERTS])
        wa_hi = sb("wa_hi", [P, 6, P], F32R)
        wa_lo = sb("wa_lo", [P, 6, P], F32R)
        sel_r = sb("sel_r", [P, 4, HG, P], F32R)
        rope_sb = sb("rope_sb", [P, 2, SEQ])
        shift_row = sb("shift_row", [P, 1])
        small = sb("small", [P, 8, GT])
        neg_half, euler, eps = small[:, 0, :], small[:, 1, :], small[:, 2, :]
        pad = small[:, 3, 0:1]
        rstd, gap, e2, share1 = small[:, 4, :], small[:, 5, :], small[:, 6, :], small[:, 7, :]

        xn = sb("xn", [P, GT, D])
        post = sb("post", [P, GT, D])
        stats = sb("stats", [P, GT, 6])
        mv = sb("mv", [P, GT, 2])
        logits = sb("logits", [P, GT, EXPERTS])
        top = sb("top", [P, GT, 8])
        top_at = sb("top_at", [P, GT, 8], U32)
        top_f = sb("top_f", [P, GT, 2])
        share2 = sb("share2", [P, GT])
        pick1 = sb("pick1", [P, GT, EXPERTS])
        gates = sb("gates", [P, GT, EXPERTS])
        gates_t = sb("gates_t", [EXPERTS, GROUP])
        mx = pick1[:, :, :].rearrange("p (t a) e -> p t (a e)", t=BT)
        rden = sb("rden", [P, HEADS])

        stage = sb("stage", [P, 2 * EXPERTS * HID])
        ring_hi = sb("ring_hi", [P, 2 * CH * GROUP], F32R)
        ring_lo = sb("ring_lo", [P, 2 * CH * GROUP], F32R)
        ring_g = sb("ring_g", [P, CH * GROUP])
        bcast = sb("bcast", [P, EXPERTS * GROUP])
        acc = sb("acc", [P, GROUP])
        tmp = sb("tmp", [P, 2, GROUP])
        x_t = post[:, :, :].rearrange("p t d -> p (t d)")

        w_raw = stage[:, :].rearrange("p (a e n) -> p a e n", a=2, e=EXPERTS)
        g_hi = ring_hi[:, :].rearrange("p (s c n) -> p s c n", s=2, c=CH)
        g_lo = ring_lo[:, :].rearrange("p (s c n) -> p s c n", s=2, c=CH)
        g_full = ring_g[:, :].rearrange("p (c n) -> p c n", c=CH)
        gate_b = bcast[:, :].rearrange("p (e n) -> p e n", e=EXPERTS)

        sel_raw = stage[:, 0:4 * HG * P]
        wa_raw = stage[:, 4 * HG * P:4 * HG * P + 6 * P]
        prob = stage[:, :].rearrange("p (u n) -> p u n", u=TU)
        qk4 = ring_hi[:, :].rearrange("p (s g m n) -> p s g m n", s=2, g=HG, m=2)
        ax_hi = x_hi[:, 0:512].rearrange("p (s n) -> p s n", s=2)
        ax_lo = x_lo[:, 0:512].rearrange("p (s n) -> p s n", s=2)
        rot_hi = x_hi[:, 512:1536].rearrange("p (s m n) -> p s m n", s=2, m=2)
        rot_lo = x_lo[:, 512:1536].rearrange("p (s m n) -> p s m n", s=2, m=2)
        qs4 = ring_lo[:, 1024:2048].rearrange("p (g n) -> p g n", g=HG)
        shift = ring_lo[:, 2048:3072]
        shift_v = shift.rearrange("p (t h c) -> p t h c", t=BT, h=HEADS)
        yt_hi = ring_lo[:, 3072:3328]
        yt_lo = ring_lo[:, 3328:3584]
        t_cos = bcast[:, 0:512].rearrange("p (m n) -> p m n", m=2)
        t_sin = bcast[:, 512:1024].rearrange("p (m n) -> p m n", m=2)
        rot = bcast[:, 1024:1536].rearrange("p (m n) -> p m n", m=2)
        y4 = bcast[:, 1536:2560].rearrange("p (g n) -> p g n", g=HG)
        y_tok = bcast[:, 2560:2816].rearrange("p (t n) -> p t n", t=BT)
        v4 = ring_g[:, :].rearrange("p (s t h c) -> p s t h c", s=2, t=BT, h=HEADS)

        x_loaded = [sem(f"x_loaded{g}") for g in range(GROUPS)]
        w_loaded = [sem(f"w_loaded{e}") for e in range(EXPERTS)]
        eye_loaded, small_loaded, att_loaded = sem("eye_loaded"), sem("small_loaded"), sem("att_loaded")
        consts_set, halved, eye_split = sem("consts_set"), sem("halved"), sem("eye_split")
        w_hi_done, w_split = sem("w_hi_done"), sem("w_split")
        def norm_sems(kind):
            return sem(f"{kind}_stats"), sem(f"{kind}_var_ready"), sem(f"{kind}_rstd_ready")

        pre_norm, post_norm, att_norm = norm_sems("pre"), norm_sems("post"), norm_sems("att")
        gate_steps, post_ready, scaled_post = sem("gate_steps"), sem("post_ready"), sem("scaled_post")
        rot_sum, rot_hi_done, rden_ready = sem("rot_sum"), sem("rot_hi_done"), sem("rden_ready")
        ln_done, xt_filled, xt_copied, xlo_done = sem("ln_done"), sem("xt_filled"), sem("xt_copied"), sem("xlo_done")
        logits_filled, gap_ready, e2_ready, gates_ready = (
            sem("logits_filled"), sem("gap_ready"), sem("e2_ready"), sem("gates_ready"))
        gt_filled, gt_copied, gt_stored, base_filled = (
            sem("gt_filled"), sem("gt_copied"), sem("gt_stored"), sem("base_filled"))
        gate_b_loaded = [sem(f"gate_b_loaded{e}") for e in range(EXPERTS)]
        tail_filled, beta_added, x_done = sem("tail_filled"), sem("beta_added"), sem("x_done")
        up_filled, gelu_done, lo_done = sem("up_filled"), sem("gelu_done"), sem("lo_done")
        down_filled, scaled, acc_done = sem("down_filled"), sem("scaled"), sem("acc_done")
        att_split, shift_zeroed, ones_set = sem("att_split"), sem("shift_zeroed"), sem("ones_set")
        a_ln_done, a_xt_filled, a_xhi_done, a_xlo_done = (
            sem("a_ln_done"), sem("a_xt_filled"), sem("a_xhi_done"), sem("a_xlo_done"))
        qk_filled, cos_done, qks_filled, sin_done, rot_ready = (
            sem("qk_filled"), sem("cos_done"), sem("qks_filled"), sem("sin_done"), sem("rot_ready"))
        v_filled, v_ready, sel_filled, qk4_ready = sem("v_filled"), sem("v_ready"), sem("sel_filled"), sem("qk4_ready")
        s_filled, max_done, shift_ready = sem("s_filled"), sem("max_done"), sem("shift_ready")
        qs_filled, qs_ready = sem("qs_filled"), sem("qs_ready")
        t_filled, exp_done = sem("t_filled"), sem("exp_done")
        pv_filled, y4_ready, yq_filled, y_ready = sem("pv_filled"), sem("y4_ready"), sem("yq_filled"), sem("y_ready")
        yt_filled, ythi_done, yt_ready, o_filled, att_done = (
            sem("yt_filled"), sem("ythi_done"), sem("yt_ready"), sem("o_filled"), sem("att_done"))
        stored = sem("stored")

        block = ctx.enter_context(nc.Block())


        def tiles(g, n=GT):
            return bass.ds(g * n, n)

        @block.sync
        def _(sp):
            def store_gates(n):
                sp.wait_ge(gt_copied, n + 1)
                sp.dma_start(gate_rows[bass.ds(n, 1), :, :].rearrange("a e n -> (a e) n"),
                             gates_t[:, :]).then_inc(gt_stored, 16)
                sp.wait_ge(gt_stored, 16 * n + 16)

            def load_gates(n, e):
                sp.dma_start(gate_b[:, e, :],
                             gate_rows[bass.ds(n, 1), e, :].broadcast_to([P, GROUP])).then_inc(gate_b_loaded[e], 16)

            def store_x(g):
                sp.wait_ge(x_done, GROUPS + g + 1)
                sp.dma_start(out[tiles(g), :, :].rearrange("t p d -> p t d"),
                             x_tok[:, tiles(g), :]).then_inc(stored, 16)

            def next_gates(phase, g):
                n = phase * GROUPS + g
                store_gates(n + 1)
                for e in range(EXPERTS):
                    sp.wait_ge(scaled, n * EXPERTS + e + 1)
                    load_gates(n + 1, e)

            sp.dma_start(x_tok[:, 0:GT, :], x[0:GT, :, :].rearrange("t p d -> p t d")).then_inc(x_loaded[0], 16)
            sp.dma_start(ident[:, :], eye).then_inc(eye_loaded, 16)
            for e in range(EXPERTS):
                sp.dma_start(w_raw[:, 0, e, :], w1[:, e, :]).then_inc(w_loaded[e], 16)
                sp.dma_start(w_raw[:, 1, e, :], w2[:, e, :]).then_inc(w_loaded[e], 16)
                if e in (1, 3, 5):
                    g = e // 2 + 1
                    sp.dma_start(x_tok[:, g * GT:(g + 1) * GT, :],
                                 x[g * GT:(g + 1) * GT, :, :].rearrange("t p d -> p t d")).then_inc(x_loaded[g], 16)
                if e == 0:
                    for dst, src in ((wg_sb[:, :], wg), (bg_sb[:, :], bg), (b1_sb[:, :, :], b1), (b2_sb[:, :], b2),
                                     (gam[:, :], gamma), (bet[:, :], beta), (iota_sb[:, :], iota8),
                                     (rope_sb[:, :, :], rope), (shift_row[:, :], ones_at)):
                        sp.dma_start(dst, src).then_inc(small_loaded, 16)
            for phase in range(2):
                store_gates(phase * GROUPS)
                for e in range(EXPERTS):
                    if phase:
                        sp.wait_ge(att_done, BATCH)
                    load_gates(phase * GROUPS, e)
                if phase == 0:
                    next_gates(0, 0)
                    sp.wait_ge(w_split, EXPERTS)
                    sp.dma_start(sel_raw, sel).then_inc(att_loaded, 16)
                    sp.dma_start(wa_raw, watt).then_inc(att_loaded, 16)
                    with sp.Fori(1, GROUPS - 1) as g:
                        next_gates(0, g)
                else:
                    next_gates(1, 0)
                    with sp.Fori(1, GROUPS - 1) as g:
                        store_x(g - 1)
                        next_gates(1, g)
                    store_x(GROUPS - 2)
                    store_x(GROUPS - 1)
            sp.wait_ge(stored, 16 * GROUPS)

        @block.gpsimd
        def _(gp):
            def rstd_of(norm, i, n):
                _, var_ready, rstd_ready = norm
                gp.wait_ge(var_ready, i + 1)
                gp.tensor_tensor(rstd[:, 0:n], mv[:, 0:n, 1], eps[:, 0:n], ALU.add).then_inc(rstd_ready, 1)
                gp.wait_ge(rstd_ready, 2 * i + 1)
                gp.tensor_tensor(rstd[:, 0:n], rstd[:, 0:n], neg_half[:, 0:n], ALU.pow).then_inc(rstd_ready, 1)

            def gate_exp(n):
                gp.wait_ge(gap_ready, n + 1)
                gp.tensor_tensor(e2[:, :], euler[:, :], gap[:, :], ALU.pow).then_inc(e2_ready, 1)

            def split_low(e):
                gp.wait_ge(w_hi_done, e + 1)
                gp.tensor_tensor(w_lo[:, :, e, :], w_raw[:, :, e, :], w_hi[:, :, e, :].bitcast(F32),
                                 ALU.subtract).then_inc(w_split, 1)

            def add_beta(n, g):
                gp.wait_ge(ln_done, n + 1)
                gp.tensor_tensor(x_tok[:, tiles(g), :], x_tok[:, tiles(g), :],
                                 bet[:, :].unsqueeze(1).broadcast_to([P, GT, D]), ALU.add).then_inc(beta_added, 1)

            def body(phase, g, first=False, last=False):
                n = phase * GROUPS + g
                for e in range(EXPERTS):
                    if e:
                        gp.wait_ge(scaled, n * EXPERTS + e + 1)
                        gp.wait_ge(acc_done, n * EXPERTS + e)
                        gp.tensor_tensor(acc[:, :], acc[:, :], tmp[:, e % 2, :], ALU.add).then_inc(acc_done, 1)
                    if first and e + 4 < EXPERTS:
                        split_low(e + 4)
                    if e == 0 and not (isinstance(g, int) and g == 0):
                        rstd_of(post_norm, n - 1, GT)
                    if e == 1 and not last:
                        rstd_of(pre_norm, n + 1, GT)
                    if e == 3:
                        add_beta(n, g)
                    if e == 5 and not last:
                        gate_exp(n + 1)
                if last:
                    rstd_of(post_norm, n, GT)

            def low_rotated(b, p):
                gp.wait_ge(rot_hi_done, b + 1)
                gp.tensor_tensor(rot_lo[:, p, :, :], rot, rot_hi[:, p, :, :].bitcast(F32),
                                 ALU.subtract).then_inc(rot_ready, 1)

            def batch(b, p, norm, more):
                if more:
                    low_rotated(b + 2, p)
                if norm:
                    rstd_of(att_norm, b + 3, BT)

            gp.memset(neg_half[:, :], -0.5).then_inc(consts_set, 1)
            gp.memset(euler[:, :], float(np.exp(1.0))).then_inc(consts_set, 1)
            gp.memset(eps[:, :], LN_EPS).then_inc(consts_set, 1)
            gp.wait_ge(consts_set, 3)
            gp.wait_ge(small_loaded, 16 * SMALL)
            gp.tensor_scalar(bet[:, :], bet[:, :], 0.5, None, ALU.mult).then_inc(halved, 1)
            gp.tensor_scalar(gam[:, :], gam[:, :], 0.5, None, ALU.mult).then_inc(halved, 1)
            gp.wait_ge(halved, 2)
            rstd_of(pre_norm, 0, GT)
            split_low(0)
            gate_exp(0)
            split_low(1)
            split_low(2)
            split_low(3)
            body(0, 0, first=True)
            with gp.Fori(1, GROUPS - 1) as g:
                body(0, g)
            body(0, GROUPS - 1, last=True)

            for b in range(3):
                rstd_of(att_norm, b, BT)
                if b < 2:
                    low_rotated(b, b)
            batch(0, 0, True, True)
            with gp.Fori(0, 2) as i:
                batch(2 * i + 1, 1, True, True)
                batch(2 * i + 2, 0, True, True)
            batch(5, 1, False, True)

            rstd_of(pre_norm, GROUPS, GT)
            gate_exp(GROUPS)
            body(1, 0)
            with gp.Fori(1, GROUPS - 1) as g:
                body(1, g)
            body(1, GROUPS - 1, last=True)

        @block.tensor
        def _(pe):
            def pass3(out_ap, wh, wl, vh, vl, start=True, stop=True):
                pe.matmul(out_ap, wh, vh, start=start, stop=False)
                pe.matmul(out_ap, wh, vl, start=False, stop=False)
                return pe.matmul(out_ap, wl, vh, start=False, stop=stop)

            def transpose_x(n):
                pe.wait_ge(ln_done, n + 1)
                for t in range(GT):
                    mm = pe.transpose(ps[:, M0, t * P:(t + 1) * P], xn[:, t, :], ident[:, :])
                mm.then_inc(xt_filled, 1)

            def router(n):
                pe.wait_ge(xt_copied, n + 1)
                for t in range(GT):
                    mm = pe.matmul(ps[:, M1, t * EXPERTS:(t + 1) * EXPERTS], x_t[:, t * P:(t + 1) * P],
                                   wg_sb[:, :], start=True, stop=True)
                mm.then_inc(logits_filled, 1)

            def transpose_gates(n):
                pe.wait_ge(gates_ready, n + 1)
                for t in range(GT):
                    mm = pe.transpose(ps[0:EXPERTS, M1, t * P:(t + 1) * P], gates[:, t, :], ident[:, :])
                mm.then_inc(gt_filled, 1)

            def base(n, g):
                pe.wait_ge(gt_copied, n + 1)
                cols = bass.ds(g * GROUP, GROUP)
                pe.matmul(ps[:, M0, :], b2_sb[:, :], gates_t[:, :], start=True, stop=False)
                pe.matmul(ps[:, M0, :], ident_r[:, :], x_hi[:, cols], start=False, stop=False)
                pe.matmul(ps[:, M0, :], ident_r[:, :], x_lo[:, cols], start=False, stop=True).then_inc(base_filled, 1)

            def up(n, g, e, split=False):
                if split:
                    pe.wait_ge(w_split, e + 1)
                if e == 0:
                    pe.wait_ge(xlo_done, n + 1)
                s = n * EXPERTS + e
                cols = bass.ds(g * GROUP, GROUP)
                for c in range(CH):
                    if not (isinstance(s, int) and s == 0):
                        pe.wait_ge(gelu_done, (s - 1) * CH + c + 1)
                    w = slice(c * P, (c + 1) * P)
                    pass3(ps[:, c, :], w_hi[:, 0, e, w], w_lo[:, 0, e, w], x_hi[:, cols], x_lo[:, cols])\
                        .then_inc(up_filled, 1)

            def down(n, e):
                s = n * EXPERTS + e
                if not (isinstance(s, int) and s < 2):
                    pe.wait_ge(scaled, s - 1)
                for c in range(CH):
                    pe.wait_ge(lo_done, s * CH + c + 1)
                    w = slice(c * P, (c + 1) * P)
                    mm = pass3(ps[:, 4 + e % 2, :], w_hi[:, 1, e, w], w_lo[:, 1, e, w],
                               g_hi[:, e % 2, c, :], g_lo[:, e % 2, c, :], c == 0, c == CH - 1)
                mm.then_inc(down_filled, 1)

            def transpose_out(n):
                pe.wait_ge(acc_done, EXPERTS * (n + 1))
                for t in range(GT):
                    mm = pe.transpose(ps[:, M1, t * P:(t + 1) * P], acc[:, t * P:(t + 1) * P], ident[:, :])
                mm.then_inc(tail_filled, 1)

            def body(phase, g, first=False, last=False):
                n = phase * GROUPS + g
                for e in range(EXPERTS):
                    down(n, e)
                    if e + 2 < EXPERTS:
                        up(n, g, e + 2, first)
                    elif not last:
                        up(n + 1, g + 1, e + 2 - EXPERTS)
                    if not last:
                        if e == 3:
                            transpose_x(n + 1)
                        if e == 4:
                            router(n + 1)
                        if e == 6:
                            transpose_gates(n + 1)
                        if e == 7:
                            base(n + 1, g + 1)
                transpose_out(n)

            def head(phase):
                n = phase * GROUPS
                transpose_x(n)
                if phase == 0:
                    pe.wait_ge(small_loaded, 16 * SMALL)
                router(n)
                up(n, 0, 0, phase == 0)
                transpose_gates(n)
                base(n, 0)
                up(n, 0, 1, phase == 0)

            def a_transpose_x(b):
                pe.wait_ge(a_ln_done, b + 1)
                for t in range(BT):
                    mm = pe.transpose(ps[:, M1, t * P:(t + 1) * P], xn[:, t, :], ident[:, :])
                mm.then_inc(a_xt_filled, 1)

            def project(p, first_w):
                for m in range(2):
                    mm = pass3(ps[:, M0, m * SEQ:(m + 1) * SEQ], wa_hi[:, first_w + m, :], wa_lo[:, first_w + m, :],
                               ax_hi[:, p, :], ax_lo[:, p, :])
                return mm

            def qk(b, p):
                pe.wait_ge(a_xlo_done, b + 1)
                project(p, 0).then_inc(qk_filled, 1)

            def qk_swapped(b, p):
                pe.wait_ge(cos_done, b + 1)
                project(p, 2).then_inc(qks_filled, 1)

            def values(b, p):
                for t in range(BT):
                    rows = slice(t * P, (t + 1) * P)
                    mm = pass3(ps[:, M0, rows], ax_hi[:, p, rows], ax_lo[:, p, rows], wa_hi[:, 4, :], wa_lo[:, 4, :])
                mm.then_inc(v_filled, 1)

            def place(b, p, g):
                if g == 0:
                    pe.wait_ge(rot_ready, b + 1)
                for m in range(2):
                    o = ps[:, M0 + g % 2, m * SEQ:(m + 1) * SEQ]
                    pe.matmul(o, sel_r[:, 2 * m, g, :], rot_hi[:, p, m, :], start=True, stop=False)
                    mm = pe.matmul(o, sel_r[:, 2 * m + 1, g, :], rot_lo[:, p, m, :], start=False, stop=True)
                mm.then_inc(sel_filled, 1)

            def scores(b, p, *us):
                for u in us:
                    pair, t, jp = u // 4, u // 2 % 2, u % 2
                    pe.wait_ge(max_done, SU * b + u + 1)
                    if u % 4 == 0:
                        pe.wait_ge(qk4_ready, 4 * b + 2 * pair + 2)
                    for gg in range(2):
                        for jj in range(2):
                            r = slice(SLOT * (2 * jp + jj), SLOT * (2 * jp + jj + 1))
                            mm = pe.matmul(ps[:, 2 * (u % 2) + jj, gg * SEQ:(gg + 1) * SEQ],
                                           qk4[r, p, 2 * pair + gg, 0, t * P:(t + 1) * P],
                                           qk4[r, p, 2 * pair + gg, 1, :], start=True, stop=True)
                    mm.then_inc(s_filled, 1)

            def place_shifted(b, p, pair):
                pe.wait_ge(shift_ready, 2 * b + pair + 1)
                for gg in range(2):
                    g = 2 * pair + gg
                    at = gg * SEQ
                    pe.matmul(ps[:, M1 - pair, at:at + SEQ], sel_r[:, 0, g, :], rot_hi[:, p, 0, :],
                              start=True, stop=False, skip_group_check=True)
                    pe.matmul(ps[:, M1 - pair, at:at + SEQ], sel_r[:, 1, g, :], rot_lo[:, p, 0, :],
                              start=False, stop=False, skip_group_check=True)
                    for t in range(BT):
                        mm = pe.matmul(ps[:, M1 - pair, at + t * P:at + (t + 1) * P],
                                       shift[:, t * 512 + g * P:t * 512 + (g + 1) * P], ident_r[:, :],
                                       start=False, stop=(t == BT - 1), skip_group_check=True)
                mm.then_inc(qs_filled, 1)

            def scores_t(b, p, *us):
                for u in us:
                    pair, t, j = u // 8, u // 4 % 2, u % 4
                    pe.wait_ge(exp_done, TU * b + u + 1)
                    if u % 8 == 0:
                        pe.wait_ge(qs_ready, 2 * b + pair + 1)
                    r = slice(SLOT * j, SLOT * (j + 1))
                    for gg in range(2):
                        g = 2 * pair + gg
                        mm = pe.matmul(ps[:, 4 + u % 2, gg * SEQ:(gg + 1) * SEQ],
                                       qk4[r, p, g, 1, t * P:(t + 1) * P], qs4[r, g, :], start=True, stop=True)
                    mm.then_inc(t_filled, 1)

            def weigh(b, p, pair):
                pe.wait_ge(exp_done, TU * b + 8 * pair + 8 + 2)
                for gg in range(2):
                    for t in range(BT):
                        for j in range(4):
                            h = 4 * (2 * pair + gg) + j
                            mm = pe.matmul(ps[SLOT * j:SLOT * (j + 1), M0 + pair, gg * SEQ:(gg + 1) * SEQ],
                                           v4[:, p, t, h, :], prob[:, 8 * pair + 4 * t + j, gg * SEQ:(gg + 1) * SEQ],
                                           start=(t == 0), stop=(t == BT - 1))
                mm.then_inc(pv_filled, 1)

            def turn_y(b, t):
                pe.wait_ge(y4_ready, 2 * b + 2)
                for g in range(HG):
                    mm = pe.transpose(ps[:, M1 - t, g * P:(g + 1) * P], y4[:, g, t * P:(t + 1) * P], ident[:, :])
                mm.then_inc(yq_filled, 1)

            def transpose_y(b):
                pe.wait_ge(y_ready, 2 * b + 2)
                for t in range(BT):
                    mm = pe.transpose(ps[:, M1, t * P:(t + 1) * P], y_tok[:, t, :], ident[:, :])
                mm.then_inc(yt_filled, 1)

            def project_out(b):
                pe.wait_ge(yt_ready, b + 1)
                for t in range(BT):
                    rows = slice(t * P, (t + 1) * P)
                    mm = pass3(ps[:, M1, rows], yt_hi[:, rows], yt_lo[:, rows], wa_hi[:, 5, :], wa_lo[:, 5, :])
                mm.then_inc(o_filled, 1)

            def batch(b, p, tail=True, place_next=True, project_next=True):
                q = 1 - p
                scores_t(b, p, 0, 1)
                if tail:
                    pe.wait_ge(att_done, b - 1)
                    weigh(b - 1, q, 1)
                if place_next:
                    pe.wait_ge(qs_ready, 2 * b + 2)
                    place(b + 1, q, 0)
                scores_t(b, p, 2, 3)
                if place_next:
                    if tail:
                        pe.wait_ge(y4_ready, 2 * b)
                    place(b + 1, q, 1)
                    pe.wait_ge(qk4_ready, 4 * b + 5)
                    place(b + 1, q, 2)
                scores_t(b, p, 4)
                if place_next:
                    scores(b + 1, q, 0)
                    pe.wait_ge(qk4_ready, 4 * b + 6)
                    place(b + 1, q, 3)
                    pe.wait_ge(qk4_ready, 4 * b + 7)
                    values(b + 1, q)
                scores_t(b, p, 5)
                if place_next:
                    scores(b + 1, q, 1)
                    pe.wait_ge(qk4_ready, 4 * b + 8)
                if tail:
                    turn_y(b - 1, 0)
                scores_t(b, p, 6)
                if place_next:
                    scores(b + 1, q, 2)
                    pe.wait_ge(v_ready, b + 2)
                if tail:
                    turn_y(b - 1, 1)
                scores_t(b, p, 7, 8)
                if place_next:
                    scores(b + 1, q, 3)
                if tail:
                    pe.wait_ge(y_ready, 2 * b - 1)
                if project_next:
                    a_transpose_x(b + 2)
                scores_t(b, p, 9)
                if tail:
                    pe.wait_ge(y_ready, 2 * b)
                weigh(b, p, 0)
                if place_next:
                    scores(b + 1, q, 4)
                if project_next:
                    pe.wait_ge(a_xlo_done, b + 3)
                if tail:
                    transpose_y(b - 1)
                scores_t(b, p, 10)
                if project_next:
                    pe.wait_ge(y4_ready, 2 * b + 1)
                    qk(b + 2, p)
                if place_next:
                    scores(b + 1, q, 5)
                    if tail:
                        pe.wait_ge(yt_ready, b)
                    place_shifted(b + 1, q, 0)
                scores_t(b, p, 11, 12)
                if place_next:
                    scores(b + 1, q, 6)
                if project_next:
                    qk_swapped(b + 2, p)
                scores_t(b, p, 13)
                if tail:
                    if place_next:
                        pe.wait_ge(qs_ready, 2 * b + 3)
                    project_out(b - 1)
                if place_next:
                    scores(b + 1, q, 7)
                scores_t(b, p, 14, 15)
                if place_next:
                    if project_next:
                        pe.wait_ge(sin_done, b + 3)
                    else:
                        pe.wait_ge(y4_ready, 2 * b + 1)
                    place_shifted(b + 1, q, 1)

            def attention():
                a_transpose_x(0)
                qk(0, 0)
                qk_swapped(0, 0)
                a_transpose_x(1)
                pe.wait_ge(sin_done, 1)
                place(0, 0, 0)
                pe.wait_ge(a_xlo_done, 2)
                place(0, 0, 1)
                pe.wait_ge(qk4_ready, 1)
                place(0, 0, 2)
                scores(0, 0, 0)
                pe.wait_ge(qk4_ready, 2)
                place(0, 0, 3)
                scores(0, 0, 1)
                pe.wait_ge(qk4_ready, 3)
                values(0, 0)
                scores(0, 0, 2)
                pe.wait_ge(v_ready, 1)
                qk(1, 1)
                scores(0, 0, 3)
                qk_swapped(1, 1)
                scores(0, 0, 4)
                pe.wait_ge(qk4_ready, 4)
                place_shifted(0, 0, 0)
                scores(0, 0, 5, 6, 7)
                pe.wait_ge(sin_done, 2)
                place_shifted(0, 0, 1)
                pe.wait_ge(qs_ready, 1)
                batch(0, 0, tail=False)
                with pe.Fori(0, 2) as i:
                    batch(2 * i + 1, 1)
                    batch(2 * i + 2, 0)
                batch(5, 1)
                batch(6, 0, project_next=False)
                batch(7, 1, place_next=False, project_next=False)
                pe.wait_ge(att_done, BATCH - 1)
                weigh(BATCH - 1, 1, 1)
                turn_y(BATCH - 1, 0)
                turn_y(BATCH - 1, 1)
                transpose_y(BATCH - 1)
                project_out(BATCH - 1)

            pe.wait_ge(eye_loaded, 16)
            pe.wait_ge(eye_split, 1)
            head(0)
            body(0, 0, first=True)
            with pe.Fori(1, GROUPS - 1) as g:
                body(0, g)
            body(0, GROUPS - 1, last=True)

            pe.wait_ge(att_split, 3)
            pe.wait_ge(shift_zeroed, 1)
            pe.wait_ge(ones_set, 1)
            attention()

            head(1)
            body(1, 0)
            with pe.Fori(1, GROUPS - 1) as g:
                body(1, g)
            body(1, GROUPS - 1, last=True)

        @block.scalar
        def _(act):
            def copy_x(n, g):
                act.wait_ge(xt_filled, n + 1)
                act.activation(x_t[:, :], ps[:, M0, :], ACT.Copy)
                act.activation(x_hi[:, bass.ds(g * GROUP, GROUP)], ps[:, M0, :], ACT.Copy).then_inc(xt_copied, 1)

            def copy_gates(n):
                act.wait_ge(gt_filled, n + 1)
                if not (isinstance(n, int) and n == 0):
                    act.wait_ge(gt_stored, 16 * n)
                act.activation(gates_t[:, :], ps[0:EXPERTS, M1, :], ACT.Copy).then_inc(gt_copied, 1)

            def gelu(n, e):
                s = n * EXPERTS + e
                if not (isinstance(s, int) and s < 2):
                    act.wait_ge(down_filled, s - 1)
                for c in range(CH):
                    act.wait_ge(up_filled, s * CH + c + 1)
                    act.activation(g_hi[:, e % 2, c, :], ps[:, c, :], ACT.Gelu, bias=b1_sb[:, e, c:c + 1])
                    if not (isinstance(s, int) and s == 0):
                        act.wait_ge(lo_done, (s - 1) * CH + c + 1)
                    act.activation(g_full[:, c, :], ps[:, c, :], ACT.Gelu, bias=b1_sb[:, e, c:c + 1])\
                        .then_inc(gelu_done, 1)

            def body(phase, g, last=False):
                n = phase * GROUPS + g
                for e in range(EXPERTS):
                    if e + 2 < EXPERTS:
                        gelu(n, e + 2)
                    elif not last:
                        gelu(n + 1, e + 2 - EXPERTS)
                    if not last:
                        if e == 3:
                            copy_x(n + 1, g + 1)
                        if e == 6:
                            copy_gates(n + 1)

            def head(phase):
                n = phase * GROUPS
                copy_x(n, 0)
                gelu(n, 0)
                copy_gates(n)
                gelu(n, 1)

            def a_copy_x(b, p):
                act.wait_ge(a_xt_filled, b + 1)
                act.activation(ax_hi[:, p, :], ps[:, M1, 0:SEQ], ACT.Copy).then_inc(a_xhi_done, 1)

            def copy_values(b, p):
                act.wait_ge(v_filled, b + 1)
                act.activation(v4[:, p, :, :, 0:HD],
                               ps[:, M0, 0:SEQ].rearrange("p (t h c) -> p t h c", t=BT, h=HEADS),
                               ACT.Copy).then_inc(v_ready, 1)

            def copy_placed(b, p, g):
                act.wait_ge(sel_filled, 4 * b + g + 1)
                act.activation(qk4[:, p, g, :, :], ps[:, M0 + g % 2, :].rearrange("p (m n) -> p m n", m=2),
                               ACT.Identity, bias=shift_row[:, :]).then_inc(qk4_ready, 1)

            def copy_shifted(b, pair):
                act.wait_ge(qs_filled, 2 * b + pair + 1)
                act.activation(qs4[:, 2 * pair:2 * pair + 2, :],
                               ps[:, M1 - pair, :].rearrange("p (g n) -> p g n", g=2), ACT.Copy).then_inc(qs_ready, 1)

            def exps(b, *us):
                for u in us:
                    act.wait_ge(t_filled, TU * b + u + 1)
                    act.activation(prob[:, u, :], ps[:, 4 + u % 2, :], ACT.Exp, scale=SCALE).then_inc(exp_done, 1)

            def copy_weighed(b, pair):
                act.wait_ge(pv_filled, 2 * b + pair + 1)
                act.activation(y4[:, 2 * pair:2 * pair + 2, :],
                               ps[:, M0 + pair, :].rearrange("p (g n) -> p g n", g=2), ACT.Copy).then_inc(y4_ready, 1)

            def copy_y(b):
                act.wait_ge(yt_filled, b + 1)
                act.activation(yt_hi, ps[:, M1, 0:SEQ], ACT.Copy).then_inc(ythi_done, 1)

            def batch(b, p, tail=True, place_next=True, project_next=True):
                q = 1 - p
                exps(b, 0, 1)
                if tail:
                    copy_weighed(b - 1, 1)
                if place_next:
                    copy_placed(b + 1, q, 0)
                exps(b, 2, 3)
                if place_next:
                    copy_placed(b + 1, q, 1)
                    copy_placed(b + 1, q, 2)
                exps(b, 4)
                if place_next:
                    copy_placed(b + 1, q, 3)
                    copy_values(b + 1, q)
                exps(b, 5, 6, 7, 8)
                if project_next:
                    a_copy_x(b + 2, p)
                exps(b, 9)
                copy_weighed(b, 0)
                if tail:
                    copy_y(b - 1)
                exps(b, 10)
                if place_next:
                    copy_shifted(b + 1, 0)
                exps(b, 11, 12, 13, 14, 15)
                if place_next:
                    copy_shifted(b + 1, 1)

            def attention():
                a_copy_x(0, 0)
                a_copy_x(1, 1)
                copy_placed(0, 0, 0)
                copy_placed(0, 0, 1)
                copy_placed(0, 0, 2)
                copy_placed(0, 0, 3)
                copy_values(0, 0)
                copy_shifted(0, 0)
                copy_shifted(0, 1)
                batch(0, 0, tail=False)
                with act.Fori(0, 2) as i:
                    batch(2 * i + 1, 1)
                    batch(2 * i + 2, 0)
                batch(5, 1)
                batch(6, 0, project_next=False)
                batch(7, 1, place_next=False, project_next=False)
                copy_weighed(BATCH - 1, 1)
                copy_y(BATCH - 1)

            act.wait_ge(small_loaded, 16 * SMALL)
            head(0)
            with act.Fori(0, GROUPS - 1) as g:
                body(0, g)
            body(0, GROUPS - 1, last=True)

            act.sem_inc(exp_done, 2)
            act.wait_ge(ones_set, 1)
            act.wait_ge(att_split, 3)
            attention()

            head(1)
            body(1, 0)
            with act.Fori(1, GROUPS - 1) as g:
                body(1, g)
            body(1, GROUPS - 1, last=True)

        @block.vector
        def _(vec):
            def norm_stats(src, count, norm, i):
                stats_done, var_ready, _ = norm
                for t in range(count):
                    vec.bn_stats(stats[:, t, :], src(t)).then_inc(stats_done, 1)
                vec.wait_ge(stats_done, (i + 1) * count)
                vec.memset(pad, 0.0)
                for t in range(count):
                    aggr = vec.bn_aggr(mv[:, t, :], stats[:, t, :])
                aggr.then_inc(var_ready, 1)

            def norm_apply(dst, src, count, norm, i):
                _, var_ready, rstd_ready = norm
                vec.wait_ge(var_ready, i + 1)
                vec.wait_ge(rstd_ready, 2 * i + 2)
                for t in range(count):
                    last = vec.tensor_scalar(dst(t), src(t), mv[:, t, 0:1], rstd[:, t:t + 1],
                                             ALU.subtract, ALU.mult)
                return last

            def x_tile(g, t, n):
                return x_tok[:, bass.ds(g * n + t, 1), :].rearrange("p a d -> p (a d)")

            def norm_in(g, n, stats_part=True, apply_part=True):
                if stats_part:
                    norm_stats(lambda t: x_tile(g, t, GT), GT, pre_norm, n)
                if apply_part:
                    norm_apply(lambda t: xn[:, t, :], lambda t: x_tile(g, t, GT), GT, pre_norm, n)\
                        .then_inc(ln_done, 1)

            def low_x(n, g):
                vec.wait_ge(xt_copied, n + 1)
                cols = bass.ds(g * GROUP, GROUP)
                vec.tensor_tensor(x_lo[:, cols], ps[:, M0, :], x_hi[:, cols].bitcast(F32),
                                  ALU.subtract).then_inc(xlo_done, 1)

            def gating(n, first_part=True, second_part=True):
                iota_b = iota_sb[:, :].unsqueeze(1).broadcast_to([P, GT, EXPERTS])
                if first_part:
                    at = Steps(n * GATE_STEPS)
                    vec.wait_ge(logits_filled, n + 1)
                    vec.tensor_tensor(logits[:, :, :], ps[:, M1, 0:GT * EXPERTS].rearrange("p (t e) -> p t e", t=GT),
                                      bg_sb[:, :].unsqueeze(1).broadcast_to([P, GT, EXPERTS]),
                                      ALU.add).then_inc(gate_steps, at.up())
                    vec.wait_ge(gate_steps, at.now())
                    vec.memset(pad, 0.0)
                    for t in range(GT):
                        op = vec.max(top[:, t, :], logits[:, t, :])
                    op.then_inc(gate_steps, at.up())
                    vec.wait_ge(gate_steps, at.now())
                    vec.tensor_tensor(gap, top[:, :, 1], top[:, :, 0], ALU.subtract).then_inc(gap_ready, 1)
                    for t in range(GT):
                        op = vec.max_index(top_at[:, t, :], top[:, t, :], logits[:, t, :])
                    op.then_inc(gate_steps, at.up())
                    vec.wait_ge(gate_steps, at.now())
                    vec.tensor_copy(top_f[:, :, :], top_at[:, :, 0:2]).then_inc(gate_steps, at.up())
                    vec.wait_ge(gate_steps, at.now())
                    vec.tensor_tensor(pick1[:, :, :], iota_b, top_f[:, :, 0:1].broadcast_to([P, GT, EXPERTS]),
                                      ALU.is_equal)
                    vec.tensor_tensor(gates[:, :, :], iota_b, top_f[:, :, 1:2].broadcast_to([P, GT, EXPERTS]),
                                      ALU.is_equal)
                if second_part:
                    at = Steps(n * GATE_STEPS + 4)
                    vec.wait_ge(e2_ready, n + 1)
                    vec.tensor_scalar(share2[:, :], e2, 1.0, None, ALU.add).then_inc(gate_steps, at.up())
                    vec.wait_ge(gate_steps, at.now())
                    vec.reciprocal(share1, share2[:, :]).then_inc(gate_steps, at.up())
                    vec.wait_ge(gate_steps, at.now())
                    vec.tensor_tensor(share2[:, :], e2, share1, ALU.mult).then_inc(gate_steps, at.up())
                    vec.tensor_tensor(pick1[:, :, :], pick1[:, :, :],
                                      share1.unsqueeze(2).broadcast_to([P, GT, EXPERTS]), ALU.mult)
                    vec.wait_ge(gate_steps, at.now())
                    vec.tensor_tensor(gates[:, :, :], gates[:, :, :],
                                      share2[:, :].unsqueeze(2).broadcast_to([P, GT, EXPERTS]),
                                      ALU.mult).then_inc(gate_steps, at.up())
                    vec.wait_ge(gate_steps, at.now())
                    vec.tensor_tensor(gates[:, :, :], gates[:, :, :], pick1[:, :, :], ALU.add).then_inc(gates_ready, 1)
                    assert 4 + at.n == GATE_STEPS

            def scale_out(n, e):
                s = n * EXPERTS + e
                vec.wait_ge(down_filled, s + 1)
                vec.wait_ge(gate_b_loaded[e], 16 * n + 16)
                if not (isinstance(s, int) and s < 2):
                    vec.wait_ge(acc_done, s - 1)
                vec.tensor_tensor(tmp[:, e % 2, :], ps[:, 4 + e % 2, :], gate_b[:, e, :],
                                  ALU.mult).then_inc(scaled, 1)
                if e == 0:
                    vec.wait_ge(scaled, s + 1)
                    vec.wait_ge(base_filled, n + 1)
                    vec.tensor_tensor(acc[:, :], ps[:, M0, :], tmp[:, 0, :], ALU.add).then_inc(acc_done, 1)

            def low_g(n, e):
                s = n * EXPERTS + e
                for c in range(CH):
                    vec.wait_ge(gelu_done, s * CH + c + 1)
                    vec.tensor_tensor(g_lo[:, e % 2, c, :], g_full[:, c, :], g_hi[:, e % 2, c, :].bitcast(F32),
                                      ALU.subtract).then_inc(lo_done, 1)

            def finish(g, n, stats_part=True, apply_part=True):
                if stats_part:
                    vec.wait_ge(tail_filled, n + 1)
                    norm_stats(lambda t: ps[:, M1, t * P:(t + 1) * P], GT, post_norm, n)
                if apply_part:
                    norm_apply(lambda t: post[:, t, :], lambda t: ps[:, M1, t * P:(t + 1) * P],
                               GT, post_norm, n).then_inc(post_ready, 1)
                    vec.wait_ge(post_ready, n + 1)
                    vec.tensor_tensor(post[:, :, :], post[:, :, :], gam[:, :].unsqueeze(1).broadcast_to([P, GT, D]),
                                      ALU.mult).then_inc(scaled_post, 1)
                    vec.wait_ge(scaled_post, n + 1)
                    vec.wait_ge(beta_added, n + 1)
                    vec.tensor_tensor(x_tok[:, tiles(g), :], x_tok[:, tiles(g), :], post[:, :, :],
                                      ALU.add).then_inc(x_done, 1)

            def split_high(e):
                vec.wait_ge(w_loaded[e], 32)
                vec.tensor_copy(w_hi[:, :, e, :], w_raw[:, :, e, :]).then_inc(w_hi_done, 1)

            def body(phase, g, first=False, last=False):
                n = phase * GROUPS + g
                for e in range(EXPERTS):
                    scale_out(n, e)
                    if e == 6 and not last:
                        gating(n + 1, first_part=False)
                    if e + 2 < EXPERTS:
                        low_g(n, e + 2)
                    elif not last:
                        low_g(n + 1, e + 2 - EXPERTS)
                    if first and e + 4 < EXPERTS:
                        split_high(e + 4)
                    behind = not (isinstance(g, int) and g == 0)
                    if e == 0 and behind:
                        finish(g - 1, n - 1, apply_part=False)
                    if e == 1 and behind:
                        finish(g - 1, n - 1, stats_part=False)
                    if not last:
                        if e == 1:
                            if first:
                                for later in x_loaded[1:]:
                                    vec.wait_ge(later, 16)
                            norm_in(g + 1, n + 1, apply_part=False)
                        if e == 2:
                            norm_in(g + 1, n + 1, stats_part=False)
                        if e == 4:
                            low_x(n + 1, g + 1)
                        if e == 5:
                            gating(n + 1, second_part=False)
                if last:
                    finish(g, n)

            def head(phase):
                n = phase * GROUPS
                norm_in(0, n)
                if phase == 0:
                    split_high(0)
                low_x(n, 0)
                if phase == 0:
                    split_high(1)
                    split_high(2)
                    vec.wait_ge(small_loaded, 16 * SMALL)
                gating(n)
                if phase == 0:
                    split_high(3)
                low_g(n, 0)
                low_g(n, 1)

            def a_norm(b, stats_part=True, apply_part=True):
                if stats_part:
                    norm_stats(lambda t: x_tile(b, t, BT), BT, att_norm, b)
                if apply_part:
                    norm_apply(lambda t: xn[:, t, :], lambda t: x_tile(b, t, BT), BT, att_norm, b)\
                        .then_inc(a_ln_done, 1)

            def a_low_x(b, p):
                vec.wait_ge(a_xhi_done, b + 1)
                vec.tensor_tensor(ax_lo[:, p, :], ps[:, M1, 0:SEQ], ax_hi[:, p, :].bitcast(F32),
                                  ALU.subtract).then_inc(a_xlo_done, 1)

            def rotate_cos(b):
                vec.wait_ge(qk_filled, b + 1)
                vec.tensor_tensor(t_cos, ps[:, M0, :].rearrange("p (m n) -> p m n", m=2),
                                  rope_sb[:, 0:1, :].broadcast_to([P, 2, SEQ]), ALU.mult).then_inc(cos_done, 1)

            def rotate_sin(b, p):
                vec.wait_ge(qks_filled, b + 1)
                vec.tensor_tensor(t_sin, ps[:, M0, :].rearrange("p (m n) -> p m n", m=2),
                                  rope_sb[:, 1:2, :].broadcast_to([P, 2, SEQ]), ALU.mult).then_inc(sin_done, 1)
                vec.wait_ge(sin_done, b + 1)
                if not (isinstance(b, int) and b == 0):
                    vec.wait_ge(rot_ready, b)
                vec.tensor_tensor(rot, t_cos, t_sin, ALU.add).then_inc(rot_sum, 1)
                vec.wait_ge(rot_sum, b + 1)
                vec.tensor_copy(rot_hi[:, p, :, :], rot).then_inc(rot_hi_done, 1)

            def maxima(b, *us):
                for u in us:
                    pair, t, jp = u // 4, u // 2 % 2, u % 2
                    vec.wait_ge(s_filled, SU * b + u + 1)
                    vec.tensor_reduce(
                        mx[:, t, :].rearrange("p (r g j) -> p r j g", r=2, g=2)[:, pair, 2 * jp:2 * jp + 2, :],
                        ps[:, 2 * (u % 2):2 * (u % 2) + 2, :].rearrange("p j (g n) -> p j g n", g=2),
                        AX.X, ALU.max).then_inc(max_done, 1)

            def negate(b, pair):
                vec.wait_ge(max_done, SU * b + 4 * pair + 4 + 2)
                vec.tensor_scalar(shift_v[:, :, 8 * pair:8 * pair + 8, 24:25].rearrange("p t h c -> p t (h c)"),
                                  mx[:, :, 8 * pair:8 * pair + 8], -1.0, None, ALU.mult).then_inc(shift_ready, 1)

            def divide(b, t):
                vec.wait_ge(yq_filled, 2 * b + t + 1)
                heads = ps[:, M1 - t, :].rearrange("p (h c) -> p h c", h=HEADS)
                if t == 1 or not (isinstance(b, int) and b == 0):
                    vec.wait_ge(y_ready, 2 * b + t)
                vec.reciprocal(rden[:, :], heads[:, :, HD]).then_inc(rden_ready, 1)
                vec.wait_ge(rden_ready, 2 * b + t + 1)
                vec.tensor_tensor(y_tok[:, t, :].rearrange("p (h c) -> p h c", h=HEADS), heads[:, :, 0:HD],
                                  rden[:, :].unsqueeze(2).broadcast_to([P, HEADS, HD]),
                                  ALU.mult).then_inc(y_ready, 1)

            def low_y(b):
                vec.wait_ge(ythi_done, b + 1)
                vec.tensor_tensor(yt_lo, ps[:, M1, 0:SEQ], yt_hi.bitcast(F32), ALU.subtract).then_inc(yt_ready, 1)

            def add_attention(b):
                vec.wait_ge(o_filled, b + 1)
                vec.tensor_tensor(x_tok[:, tiles(b, BT), :], ps[:, M1, 0:SEQ].rearrange("p (t d) -> p t d", t=BT),
                                  x_tok[:, tiles(b, BT), :], ALU.add).then_inc(att_done, 1)

            def batch(b, p, tail=True, place_next=True, project_next=True, norm=True):
                if place_next:
                    maxima(b + 1, 0, 1)
                if tail:
                    divide(b - 1, 0)
                if place_next:
                    maxima(b + 1, 2)
                if tail:
                    divide(b - 1, 1)
                if place_next:
                    maxima(b + 1, 3)
                    negate(b + 1, 0)
                if project_next:
                    a_low_x(b + 2, p)
                if place_next:
                    maxima(b + 1, 4)
                if tail:
                    low_y(b - 1)
                if project_next:
                    rotate_cos(b + 2)
                if place_next:
                    maxima(b + 1, 5, 6)
                if project_next:
                    rotate_sin(b + 2, p)
                if norm:
                    a_norm(b + 3, apply_part=False)
                if tail:
                    add_attention(b - 1)
                if place_next:
                    maxima(b + 1, 7)
                    negate(b + 1, 1)
                if norm:
                    a_norm(b + 3, stats_part=False)

            def attention():
                vec.wait_ge(x_done, GROUPS)
                a_norm(0)
                a_low_x(0, 0)
                rotate_cos(0)
                rotate_sin(0, 0)
                a_norm(1)
                a_low_x(1, 1)
                maxima(0, 0, 1, 2)
                rotate_cos(1)
                maxima(0, 3)
                negate(0, 0)
                rotate_sin(1, 1)
                a_norm(2)
                maxima(0, 4, 5, 6, 7)
                negate(0, 1)
                batch(0, 0, tail=False)
                with vec.Fori(0, 2) as i:
                    batch(2 * i + 1, 1)
                    batch(2 * i + 2, 0)
                batch(5, 1, norm=False)
                batch(6, 0, project_next=False, norm=False)
                batch(7, 1, place_next=False, project_next=False, norm=False)
                divide(BATCH - 1, 0)
                divide(BATCH - 1, 1)
                low_y(BATCH - 1)
                add_attention(BATCH - 1)

            vec.wait_ge(eye_loaded, 16)
            vec.tensor_copy(ident_r[:, :], ident[:, :]).then_inc(eye_split, 1)
            vec.wait_ge(x_loaded[0], 16)
            head(0)
            body(0, 0, first=True)
            with vec.Fori(1, GROUPS - 1) as g:
                body(0, g)
            body(0, GROUPS - 1, last=True)

            vec.wait_ge(att_loaded, 32)
            vec.tensor_copy(sel_r[:, :, :, :].rearrange("p a g m -> p (a g m)"), sel_raw).then_inc(att_split, 1)
            vec.tensor_copy(wa_hi[:, :, :].rearrange("p a m -> p (a m)"), wa_raw).then_inc(att_split, 1)
            vec.wait_ge(att_split, 2)
            vec.tensor_tensor(wa_lo[:, :, :].rearrange("p a m -> p (a m)"), wa_raw,
                              wa_hi[:, :, :].rearrange("p a m -> p (a m)").bitcast(F32),
                              ALU.subtract).then_inc(att_split, 1)
            vec.memset(ring_g[:, :], 1.0).then_inc(ones_set, 1)
            vec.memset(shift.bitcast(F32), 0.0).then_inc(shift_zeroed, 1)
            vec.sem_inc(max_done, 2)
            attention()

            head(1)
            body(1, 0)
            with vec.Fori(1, GROUPS - 1) as g:
                body(1, g)
            body(1, GROUPS - 1, last=True)


def shape_constants():
    pair = np.arange(HD // 2, dtype=np.float32)
    angle = np.power(np.float32(10000.0), np.float32(2.0) * pair / np.float32(HD)).astype(np.float32)
    theta = (np.arange(SEQ, dtype=np.float32)[:, None] * angle[None, :]).astype(np.float32)
    cos, sin = np.cos(theta).astype(np.float32), np.sin(theta).astype(np.float32)
    rope = np.zeros((P, 2, SEQ), np.float32)
    for c in range(P):
        rope[c, 0] = cos[:, c % HD // 2]
        rope[c, 1] = sin[:, c % HD // 2] * (1 if c % 2 else -1)
    sel = np.zeros((P, 4, HG, P), np.float32)
    parts = ((0, 2), (1,), (0, 1), (2,))
    for kind, eights in enumerate(parts):
        for h in range(HEADS):
            g, j = h // 4, h % 4
            for r in eights:
                for c in range(HD):
                    sel[HD * h + c, kind, g, SLOT * j + HD * r + c] = 1.0
    ones_at = np.zeros((P, 1), np.float32)
    ones_at[24::SLOT] = 1.0
    iota8 = np.ascontiguousarray(np.broadcast_to(np.arange(EXPERTS, dtype=np.float32), (P, EXPERTS)))
    return dict(rope=rope, sel=sel.reshape(P, -1), ones_at=ones_at, eye=np.eye(P, dtype=np.float32), iota8=iota8)


def kernel(L0_attn_x, L0_attn_w_q, L0_attn_w_k, L0_attn_w_v, L0_attn_w_o, L0_ffn_Wg, L0_ffn_bg, L0_ffn_W1,
           L0_ffn_b1, L0_ffn_W2, L0_ffn_b2, L0_ffn_gamma, L0_ffn_beta):
    import concourse.bacc as bacc
    from concourse.bass_utils import run_bass_kernel_spmd

    def rows(a):
        a = np.asarray(a)
        return np.ascontiguousarray(np.broadcast_to(a, (P,) + a.shape))

    swap = np.arange(P).reshape(-1, 2)[:, ::-1].reshape(-1)
    wq, wk, wv, wo = (np.asarray(w) for w in (L0_attn_w_q, L0_attn_w_k, L0_attn_w_v, L0_attn_w_o))
    w1, w2 = np.asarray(L0_ffn_W1), np.asarray(L0_ffn_W2)
    arrays = dict(
        x=np.asarray(L0_attn_x).reshape(TILES, P, D),
        w1=w1.transpose(1, 0, 2),
        w2=w2.reshape(EXPERTS, CH, P, D).transpose(2, 0, 1, 3).reshape(P, EXPERTS, HID),
        wg=np.asarray(L0_ffn_Wg),
        bg=rows(L0_ffn_bg),
        b1=np.asarray(L0_ffn_b1).reshape(EXPERTS, CH, P).transpose(2, 0, 1),
        b2=np.asarray(L0_ffn_b2),
        gamma=rows(L0_ffn_gamma),
        beta=rows(L0_ffn_beta),
        watt=np.stack([wq.T, wk.T, wq[swap].T, wk[swap].T, wv.T, wo.T], axis=1).reshape(P, 6 * P),
        **shape_constants(),
    )
    arrays = {n: np.ascontiguousarray(a) for n, a in arrays.items()}
    nc = bacc.Bacc("TRN2", target_bir_lowering=False, num_devices=1)
    args = {n: nc.dram_tensor(n, a.shape, mybir.dt.from_np(a.dtype), kind="ExternalInput").ap()
            for n, a in arrays.items()}
    args["out"] = nc.dram_tensor("out", (TILES, P, D), F32, kind="ExternalOutput").ap()
    build(nc, **args)
    result = run_bass_kernel_spmd(nc, [arrays], core_ids=[0])
    return result.results[0]["out"].reshape(BATCH, SEQ, D)
```

```python
from contextlib import ExitStack

import concourse.bass as bass
import numpy as np
from concourse import mybir

F32 = mybir.dt.float32
F32R = mybir.dt.float32r
U32 = mybir.dt.uint32
ALU = mybir.AluOpType
ACT = mybir.ActivationFunctionType
AX = mybir.AxisListType

P = 128
BATCH, SEQ, D = 8, 256, 128
HEADS, HD = 16, 8
EXPERTS, HID = 8, 512
LN_EPS = 1e-5
TOKENS = BATCH * SEQ
TILES = TOKENS // P
GROUP = 512
GROUPS = TOKENS // GROUP
GT = GROUP // P
CH = HID // P
BT = SEQ // P
HG = 4
SLOT = P // HG
TU = 16
SU = 8
SCALE = HD ** -0.5
SMALL = 9
M0, M1 = 6, 7


class Steps:

    def __init__(self, base):
        self.base, self.n = base, 0

    def up(self):
        self.n += 1
        return 1

    def now(self):
        return self.base + self.n


GATE_STEPS = 8
CLOCK_UNITS = (0, 2, 4, 9, 10, 12)
START_SCORES, START_SCORES_T = 1, 1


def build(nc, x, w1, w2, wg, bg, b1, b2, gamma, beta, watt, rope, sel, ones_at, eye, iota8, out):
    with ExitStack() as ctx:
        def sb(name, shape, dt=F32):
            return ctx.enter_context(nc.sbuf_tensor(name, shape, dt))

        def sem(name):
            return ctx.enter_context(nc.semaphore(name))

        ps = ctx.enter_context(nc.psum_tensor("ps", [P, 8, 512], F32))
        gate_rows = nc.dram_tensor("gate_rows", [2 * GROUPS, EXPERTS, GROUP], F32, kind="Internal").ap()

        x_tok = sb("x_tok", [P, TILES, D])
        w_hi = sb("w_hi", [P, 2, EXPERTS, HID], F32R)
        w_lo = sb("w_lo", [P, 2, EXPERTS, HID], F32R)
        x_hi = sb("x_hi", [P, TOKENS], F32R)
        x_lo = sb("x_lo", [P, TOKENS], F32R)
        ident = sb("ident", [P, P])
        ident_r = sb("ident_r", [P, P], F32R)
        wg_sb = sb("wg_sb", [P, EXPERTS])
        bg_sb = sb("bg_sb", [P, EXPERTS])
        b1_sb = sb("b1_sb", [P, EXPERTS, CH])
        b2_sb = sb("b2_sb", [EXPERTS, D])
        gam = sb("gam", [P, D])
        bet = sb("bet", [P, D])
        iota_sb = sb("iota_sb", [P, EXPERTS])
        wa_hi = sb("wa_hi", [P, 6, P], F32R)
        wa_lo = sb("wa_lo", [P, 6, P], F32R)
        sel_r = sb("sel_r", [P, 4, HG, P], F32R)
        rope_sb = sb("rope_sb", [P, 2, SEQ])
        shift_row = sb("shift_row", [P, 1])
        small = sb("small", [P, 8, GT])
        neg_half, euler, eps = small[:, 0, :], small[:, 1, :], small[:, 2, :]
        pad = small[:, 3, 0:1]
        rstd, gap, e2, share1 = small[:, 4, :], small[:, 5, :], small[:, 6, :], small[:, 7, :]

        xn = sb("xn", [P, GT, D])
        post = sb("post", [P, GT, D])
        stats = sb("stats", [P, GT, 6])
        mv = sb("mv", [P, GT, 2])
        logits = sb("logits", [P, GT, EXPERTS])
        top = sb("top", [P, GT, 8])
        top_at = sb("top_at", [P, GT, 8], U32)
        top_f = sb("top_f", [P, GT, 2])
        share2 = sb("share2", [P, GT])
        pick1 = sb("pick1", [P, GT, EXPERTS])
        gates = sb("gates", [P, GT, EXPERTS])
        gates_t = sb("gates_t", [EXPERTS, GROUP])
        mx = pick1[:, :, :].rearrange("p (t a) e -> p t (a e)", t=BT)
        rden = sb("rden", [P, HEADS])

        stage = sb("stage", [P, 2 * EXPERTS * HID])
        ring_hi = sb("ring_hi", [P, 2 * CH * GROUP], F32R)
        ring_lo = sb("ring_lo", [P, 2 * CH * GROUP], F32R)
        ring_g = sb("ring_g", [P, CH * GROUP])
        bcast = sb("bcast", [P, EXPERTS * GROUP])
        acc = sb("acc", [P, GROUP])
        tmp = sb("tmp", [P, 2, GROUP])
        x_t = post[:, :, :].rearrange("p t d -> p (t d)")

        w_raw = stage[:, :].rearrange("p (a e n) -> p a e n", a=2, e=EXPERTS)
        g_hi = ring_hi[:, :].rearrange("p (s c n) -> p s c n", s=2, c=CH)
        g_lo = ring_lo[:, :].rearrange("p (s c n) -> p s c n", s=2, c=CH)
        g_full = ring_g[:, :].rearrange("p (c n) -> p c n", c=CH)
        gate_b = bcast[:, :].rearrange("p (e n) -> p e n", e=EXPERTS)

        sel_raw = stage[:, 0:4 * HG * P]
        wa_raw = stage[:, 4 * HG * P:4 * HG * P + 6 * P]
        prob = stage[:, :].rearrange("p (u n) -> p u n", u=TU)
        qk4 = ring_hi[:, :].rearrange("p (s g m n) -> p s g m n", s=2, g=HG, m=2)
        ax_hi = x_hi[:, 0:512].rearrange("p (s n) -> p s n", s=2)
        ax_lo = x_lo[:, 0:512].rearrange("p (s n) -> p s n", s=2)
        rot_hi = x_hi[:, 512:1536].rearrange("p (s m n) -> p s m n", s=2, m=2)
        rot_lo = x_lo[:, 512:1536].rearrange("p (s m n) -> p s m n", s=2, m=2)
        qs4 = ring_lo[:, 1024:2048].rearrange("p (g n) -> p g n", g=HG)
        shift = ring_lo[:, 2048:3072]
        shift_v = shift.rearrange("p (t h c) -> p t h c", t=BT, h=HEADS)
        yt_hi = ring_lo[:, 3072:3328]
        yt_lo = ring_lo[:, 3328:3584]
        t_cos = bcast[:, 0:512].rearrange("p (m n) -> p m n", m=2)
        t_sin = bcast[:, 512:1024].rearrange("p (m n) -> p m n", m=2)
        rot = bcast[:, 1024:1536].rearrange("p (m n) -> p m n", m=2)
        y4 = bcast[:, 1536:2560].rearrange("p (g n) -> p g n", g=HG)
        y_tok = bcast[:, 2560:2816].rearrange("p (t n) -> p t n", t=BT)
        v4 = ring_g[:, :].rearrange("p (s t h c) -> p s t h c", s=2, t=BT, h=HEADS)

        x_loaded = [sem(f"x_loaded{g}") for g in range(GROUPS)]
        w_loaded = [sem(f"w_loaded{e}") for e in range(EXPERTS)]
        eye_loaded, small_loaded, att_loaded = sem("eye_loaded"), sem("small_loaded"), sem("att_loaded")
        consts_set, halved, eye_split = sem("consts_set"), sem("halved"), sem("eye_split")
        w_hi_done, w_split = sem("w_hi_done"), sem("w_split")
        def norm_sems(kind):
            return sem(f"{kind}_stats"), sem(f"{kind}_var_ready"), sem(f"{kind}_rstd_ready")

        pre_norm, post_norm, att_norm = norm_sems("pre"), norm_sems("post"), norm_sems("att")
        gate_steps, post_ready, scaled_post = sem("gate_steps"), sem("post_ready"), sem("scaled_post")
        rot_sum, rot_hi_done, rden_ready = sem("rot_sum"), sem("rot_hi_done"), sem("rden_ready")
        ln_done, xt_filled, xt_copied, xlo_done = sem("ln_done"), sem("xt_filled"), sem("xt_copied"), sem("xlo_done")
        logits_filled, gap_ready, e2_ready, gates_ready = (
            sem("logits_filled"), sem("gap_ready"), sem("e2_ready"), sem("gates_ready"))
        gt_filled, gt_copied, gt_stored, base_filled = (
            sem("gt_filled"), sem("gt_copied"), sem("gt_stored"), sem("base_filled"))
        gate_b_loaded = [sem(f"gate_b_loaded{e}") for e in range(EXPERTS)]
        tail_filled, beta_added, x_done = sem("tail_filled"), sem("beta_added"), sem("x_done")
        up_filled, gelu_done, lo_done = sem("up_filled"), sem("gelu_done"), sem("lo_done")
        down_filled, scaled, acc_done = sem("down_filled"), sem("scaled"), sem("acc_done")
        att_split, shift_zeroed, ones_set = sem("att_split"), sem("shift_zeroed"), sem("ones_set")
        a_ln_done, a_xt_filled, a_xhi_done, a_xlo_done = (
            sem("a_ln_done"), sem("a_xt_filled"), sem("a_xhi_done"), sem("a_xlo_done"))
        qk_filled, cos_done, qks_filled, sin_done, rot_ready = (
            sem("qk_filled"), sem("cos_done"), sem("qks_filled"), sem("sin_done"), sem("rot_ready"))
        v_filled, v_ready, sel_filled, qk4_ready = sem("v_filled"), sem("v_ready"), sem("sel_filled"), sem("qk4_ready")
        s_filled, max_done, shift_ready = sem("s_filled"), sem("max_done"), sem("shift_ready")
        qs_filled, qs_ready = sem("qs_filled"), sem("qs_ready")
        t_filled, exp_done = sem("t_filled"), sem("exp_done")
        pv_filled, y4_ready, yq_filled, y_ready = sem("pv_filled"), sem("y4_ready"), sem("yq_filled"), sem("y_ready")
        yt_filled, ythi_done, yt_ready, o_filled, att_done = (
            sem("yt_filled"), sem("ythi_done"), sem("yt_ready"), sem("o_filled"), sem("att_done"))
        stored = sem("stored")

        block = ctx.enter_context(nc.Block())


        def tiles(g, n=GT):
            return bass.ds(g * n, n)

        @block.sync
        def _(sp):
            def store_gates(n):
                sp.wait_ge(gt_copied, n + 1)
                sp.dma_start(gate_rows[bass.ds(n, 1), :, :].rearrange("a e n -> (a e) n"),
                             gates_t[:, :]).then_inc(gt_stored, 16)
                sp.wait_ge(gt_stored, 16 * n + 16)

            def load_gates(n, e):
                sp.dma_start(gate_b[:, e, :],
                             gate_rows[bass.ds(n, 1), e, :].broadcast_to([P, GROUP])).then_inc(gate_b_loaded[e], 16)

            def store_x(g):
                sp.wait_ge(x_done, GROUPS + g + 1)
                sp.dma_start(out[tiles(g), :, :].rearrange("t p d -> p t d"),
                             x_tok[:, tiles(g), :]).then_inc(stored, 16)

            def next_gates(phase, g):
                n = phase * GROUPS + g
                store_gates(n + 1)
                for e in range(EXPERTS):
                    sp.wait_ge(scaled, n * EXPERTS + e + 1)
                    load_gates(n + 1, e)

            sp.dma_start(x_tok[:, 0:GT, :], x[0:GT, :, :].rearrange("t p d -> p t d")).then_inc(x_loaded[0], 16)
            sp.dma_start(ident[:, :], eye).then_inc(eye_loaded, 16)
            for e in range(EXPERTS):
                sp.dma_start(w_raw[:, 0, e, :], w1[:, e, :]).then_inc(w_loaded[e], 16)
                sp.dma_start(w_raw[:, 1, e, :], w2[:, e, :]).then_inc(w_loaded[e], 16)
                if e in (1, 3, 5):
                    g = e // 2 + 1
                    sp.dma_start(x_tok[:, g * GT:(g + 1) * GT, :],
                                 x[g * GT:(g + 1) * GT, :, :].rearrange("t p d -> p t d")).then_inc(x_loaded[g], 16)
                if e == 0:
                    for dst, src in ((wg_sb[:, :], wg), (bg_sb[:, :], bg), (b1_sb[:, :, :], b1), (b2_sb[:, :], b2),
                                     (gam[:, :], gamma), (bet[:, :], beta), (iota_sb[:, :], iota8),
                                     (rope_sb[:, :, :], rope), (shift_row[:, :], ones_at)):
                        sp.dma_start(dst, src).then_inc(small_loaded, 16)
            for phase in range(2):
                store_gates(phase * GROUPS)
                for e in range(EXPERTS):
                    if phase and e == 3:
                        sp.wait_ge(att_done, BATCH + 1)
                    load_gates(phase * GROUPS, e)
                if phase == 0:
                    next_gates(0, 0)
                    sp.wait_ge(w_split, EXPERTS)
                    sp.dma_start(sel_raw, sel).then_inc(att_loaded, 16)
                    sp.dma_start(wa_raw, watt).then_inc(att_loaded, 16)
                    with sp.Fori(1, GROUPS - 1) as g:
                        next_gates(0, g)
                else:
                    next_gates(1, 0)
                    with sp.Fori(1, GROUPS - 1) as g:
                        store_x(g - 1)
                        next_gates(1, g)
                    store_x(GROUPS - 2)
                    store_x(GROUPS - 1)
            sp.wait_ge(stored, 16 * GROUPS)

        @block.gpsimd
        def _(gp):
            def rstd_of(norm, i, n):
                _, var_ready, rstd_ready = norm
                gp.wait_ge(var_ready, i + 1)
                gp.tensor_tensor(rstd[:, 0:n], mv[:, 0:n, 1], eps[:, 0:n], ALU.add).then_inc(rstd_ready, 1)
                gp.wait_ge(rstd_ready, 2 * i + 1)
                gp.tensor_tensor(rstd[:, 0:n], rstd[:, 0:n], neg_half[:, 0:n], ALU.pow).then_inc(rstd_ready, 1)

            def gate_exp(n):
                gp.wait_ge(gap_ready, n + 1)
                gp.tensor_tensor(e2[:, :], euler[:, :], gap[:, :], ALU.pow).then_inc(e2_ready, 1)

            def split_low(e):
                gp.wait_ge(w_hi_done, e + 1)
                gp.tensor_tensor(w_lo[:, :, e, :], w_raw[:, :, e, :], w_hi[:, :, e, :].bitcast(F32),
                                 ALU.subtract).then_inc(w_split, 1)

            def add_beta(n, g):
                gp.wait_ge(ln_done, n + 1)
                gp.tensor_tensor(x_tok[:, tiles(g), :], x_tok[:, tiles(g), :],
                                 bet[:, :].unsqueeze(1).broadcast_to([P, GT, D]), ALU.add).then_inc(beta_added, 1)

            def low_rotated(b, p):
                gp.wait_ge(rot_hi_done, b + 1)
                gp.tensor_tensor(rot_lo[:, p, :, :], rot, rot_hi[:, p, :, :].bitcast(F32),
                                 ALU.subtract).then_inc(rot_ready, 1)

            def body(phase, g, first=False, last=False):
                n = phase * GROUPS + g
                for e in range(EXPERTS):
                    if e:
                        gp.wait_ge(scaled, n * EXPERTS + e + 1)
                        gp.wait_ge(acc_done, n * EXPERTS + e)
                        gp.tensor_tensor(acc[:, :], acc[:, :], tmp[:, e % 2, :], ALU.add).then_inc(acc_done, 1)
                    if first and e + 4 < EXPERTS:
                        split_low(e + 4)
                    if e == 0 and not (isinstance(g, int) and g == 0):
                        rstd_of(post_norm, n - 1, GT)
                    if e == 1 and not last:
                        rstd_of(pre_norm, n + 1, GT)
                    if e == 3:
                        add_beta(n, g)
                    if e == 5 and not last:
                        gate_exp(n + 1)
                    if last and phase == 0:
                        if e in (1, 3):
                            rstd_of(att_norm, e // 2, BT)
                        if e == 6:
                            low_rotated(0, 0)
                        if e == 7:
                            low_rotated(1, 1)
                if last:
                    rstd_of(post_norm, n, GT)

            def batch(b, p, norm, more):
                if more:
                    low_rotated(b + 2, p)
                if norm:
                    rstd_of(att_norm, b + 3, BT)

            gp.memset(neg_half[:, :], -0.5).then_inc(consts_set, 1)
            gp.memset(euler[:, :], float(np.exp(1.0))).then_inc(consts_set, 1)
            gp.memset(eps[:, :], LN_EPS).then_inc(consts_set, 1)
            gp.wait_ge(consts_set, 3)
            rstd_of(pre_norm, 0, GT)
            gp.wait_ge(small_loaded, 16 * SMALL)
            gp.tensor_scalar(bet[:, :], bet[:, :], 0.5, None, ALU.mult).then_inc(halved, 1)
            gp.tensor_scalar(gam[:, :], gam[:, :], 0.5, None, ALU.mult).then_inc(halved, 1)
            gp.wait_ge(halved, 2)
            split_low(0)
            gate_exp(0)
            split_low(1)
            split_low(2)
            split_low(3)
            body(0, 0, first=True)
            with gp.Fori(1, GROUPS - 1) as g:
                body(0, g)
            body(0, GROUPS - 1, last=True)

            gp.wait_ge(lo_done, GROUPS * EXPERTS * CH)
            gp.memset(ring_g[:, :], 1.0).then_inc(ones_set, 1)
            gp.wait_ge(down_filled, GROUPS * EXPERTS)
            gp.memset(shift.bitcast(F32), 0.0).then_inc(shift_zeroed, 1)
            rstd_of(att_norm, 2, BT)
            batch(0, 0, True, True)
            with gp.Fori(0, 2) as i:
                batch(2 * i + 1, 1, True, True)
                batch(2 * i + 2, 0, True, True)
            batch(5, 1, False, True)

            rstd_of(pre_norm, GROUPS, GT)
            gate_exp(GROUPS)
            body(1, 0)
            with gp.Fori(1, GROUPS - 1) as g:
                body(1, g)
            body(1, GROUPS - 1, last=True)

        @block.tensor
        def _(pe):
            def pass3(out_ap, wh, wl, vh, vl, start=True, stop=True):
                pe.matmul(out_ap, wh, vh, start=start, stop=False)
                pe.matmul(out_ap, wh, vl, start=False, stop=False)
                return pe.matmul(out_ap, wl, vh, start=False, stop=stop)

            def transpose_x(n, bank=M0):
                pe.wait_ge(ln_done, n + 1)
                for t in range(GT):
                    mm = pe.transpose(ps[:, bank, t * P:(t + 1) * P], xn[:, t, :], ident[:, :])
                mm.then_inc(xt_filled, 1)

            def router(n, bank=M1):
                pe.wait_ge(xt_copied, n + 1)
                for t in range(GT):
                    mm = pe.matmul(ps[:, bank, t * EXPERTS:(t + 1) * EXPERTS], x_t[:, t * P:(t + 1) * P],
                                   wg_sb[:, :], start=True, stop=True)
                mm.then_inc(logits_filled, 1)

            def transpose_gates(n, bank=M1):
                pe.wait_ge(gates_ready, n + 1)
                for t in range(GT):
                    mm = pe.transpose(ps[0:EXPERTS, bank, t * P:(t + 1) * P], gates[:, t, :], ident[:, :])
                mm.then_inc(gt_filled, 1)

            def base(n, g):
                pe.wait_ge(gt_copied, n + 1)
                cols = bass.ds(g * GROUP, GROUP)
                pe.matmul(ps[:, M0, :], b2_sb[:, :], gates_t[:, :], start=True, stop=False)
                pe.matmul(ps[:, M0, :], ident_r[:, :], x_hi[:, cols], start=False, stop=False)
                pe.matmul(ps[:, M0, :], ident_r[:, :], x_lo[:, cols], start=False, stop=True).then_inc(base_filled, 1)

            def up(n, g, e, split=False):
                if split:
                    pe.wait_ge(w_split, e + 1)
                if e == 0:
                    pe.wait_ge(xlo_done, n + 1)
                s = n * EXPERTS + e
                cols = bass.ds(g * GROUP, GROUP)
                for c in range(CH):
                    if not (isinstance(s, int) and s == 0):
                        pe.wait_ge(gelu_done, (s - 1) * CH + c + 1)
                    w = slice(c * P, (c + 1) * P)
                    pass3(ps[:, c, :], w_hi[:, 0, e, w], w_lo[:, 0, e, w], x_hi[:, cols], x_lo[:, cols])\
                        .then_inc(up_filled, 1)

            def down(n, e):
                s = n * EXPERTS + e
                if not (isinstance(s, int) and s < 2):
                    pe.wait_ge(scaled, s - 1)
                for c in range(CH):
                    pe.wait_ge(lo_done, s * CH + c + 1)
                    w = slice(c * P, (c + 1) * P)
                    mm = pass3(ps[:, 4 + e % 2, :], w_hi[:, 1, e, w], w_lo[:, 1, e, w],
                               g_hi[:, e % 2, c, :], g_lo[:, e % 2, c, :], c == 0, c == CH - 1)
                mm.then_inc(down_filled, 1)

            def transpose_out(n, bank=M1):
                pe.wait_ge(acc_done, EXPERTS * (n + 1))
                for t in range(GT):
                    mm = pe.transpose(ps[:, bank, t * P:(t + 1) * P], acc[:, t * P:(t + 1) * P], ident[:, :])
                mm.then_inc(tail_filled, 1)

            def a_transpose_x(b):
                pe.wait_ge(a_ln_done, b + 1)
                for t in range(BT):
                    mm = pe.transpose(ps[:, M1, t * P:(t + 1) * P], xn[:, t, :], ident[:, :])
                mm.then_inc(a_xt_filled, 1)

            def project(p, first_w):
                for m in range(2):
                    mm = pass3(ps[:, M0, m * SEQ:(m + 1) * SEQ], wa_hi[:, first_w + m, :], wa_lo[:, first_w + m, :],
                               ax_hi[:, p, :], ax_lo[:, p, :])
                return mm

            def qk(b, p):
                pe.wait_ge(a_xlo_done, b + 1)
                project(p, 0).then_inc(qk_filled, 1)

            def qk_swapped(b, p):
                pe.wait_ge(cos_done, b + 1)
                project(p, 2).then_inc(qks_filled, 1)

            def values(b, p):
                for t in range(BT):
                    rows = slice(t * P, (t + 1) * P)
                    mm = pass3(ps[:, M0, rows], ax_hi[:, p, rows], ax_lo[:, p, rows], wa_hi[:, 4, :], wa_lo[:, 4, :])
                mm.then_inc(v_filled, 1)

            def start_attention(e):
                if e == 3:
                    a_transpose_x(0)
                if e == 5:
                    pe.wait_ge(att_split, 3)
                    qk(0, 0)
                    a_transpose_x(1)
                if e == 6:
                    qk_swapped(0, 0)
                if e == 7:
                    pe.wait_ge(sin_done, 1)
                    qk(1, 1)

            def body(phase, g, first=False, last=False):
                n = phase * GROUPS + g
                for e in range(EXPERTS):
                    down(n, e)
                    if e == 0 and not (isinstance(g, int) and g == 0):
                        transpose_out(n - 1)
                    if e == 4 and not last:
                        transpose_x(n + 1)
                    if e + 2 < EXPERTS:
                        up(n, g, e + 2, first)
                    elif not last:
                        up(n + 1, g + 1, e + 2 - EXPERTS)
                    if not last:
                        if e == 4:
                            router(n + 1)
                        if e == 6:
                            transpose_gates(n + 1)
                        if e == 7:
                            base(n + 1, g + 1)
                    elif phase == 0:
                        start_attention(e)
                if last and phase:
                    transpose_out(n)

            def first_head():
                transpose_x(0)
                pe.wait_ge(small_loaded, 16 * SMALL)
                router(0)
                up(0, 0, 0, True)
                transpose_gates(0)
                base(0, 0)
                up(0, 0, 1, True)

            def second_head():
                pe.wait_ge(gt_copied, GROUPS + 1)
                up(GROUPS, 0, 0)
                base(GROUPS, 0)
                up(GROUPS, 0, 1)

            def place(b, p, g):
                if g == 0:
                    pe.wait_ge(rot_ready, b + 1)
                for m in range(2):
                    o = ps[:, M1 - g % 2, m * SEQ:(m + 1) * SEQ]
                    pe.matmul(o, sel_r[:, 2 * m, g, :], rot_hi[:, p, m, :], start=True, stop=False)
                    mm = pe.matmul(o, sel_r[:, 2 * m + 1, g, :], rot_lo[:, p, m, :], start=False, stop=True)
                mm.then_inc(sel_filled, 1)

            def keep_clock(bank, times):
                for _ in range(times):
                    pe.matmul(ps[:, bank, :], ident_r[:, :], sel_r[:, 0, :, :], start=True, stop=True)

            def scores(b, p, *us):
                for u in us:
                    pair, t, jp = u // 4, u // 2 % 2, u % 2
                    pe.wait_ge(max_done, SU * b + u + 1)
                    if u % 4 == 0:
                        pe.wait_ge(qk4_ready, 4 * b + 2 * pair + 2)
                    if isinstance(b, int) and b == 0:
                        keep_clock(2 * (u % 2), START_SCORES)
                    for gg in range(2):
                        for jj in range(2):
                            r = slice(SLOT * (2 * jp + jj), SLOT * (2 * jp + jj + 1))
                            mm = pe.matmul(ps[:, 2 * (u % 2) + jj, gg * SEQ:(gg + 1) * SEQ],
                                           qk4[r, p, 2 * pair + gg, 0, t * P:(t + 1) * P],
                                           qk4[r, p, 2 * pair + gg, 1, :], start=True, stop=True)
                    mm.then_inc(s_filled, 1)

            def place_shifted(b, p, pair):
                pe.wait_ge(shift_ready, 2 * b + pair + 1)
                for gg in range(2):
                    g = 2 * pair + gg
                    at = gg * SEQ
                    pe.matmul(ps[:, M1 - pair, at:at + SEQ], sel_r[:, 0, g, :], rot_hi[:, p, 0, :],
                              start=True, stop=False, skip_group_check=True)
                    pe.matmul(ps[:, M1 - pair, at:at + SEQ], sel_r[:, 1, g, :], rot_lo[:, p, 0, :],
                              start=False, stop=False, skip_group_check=True)
                    for t in range(BT):
                        mm = pe.matmul(ps[:, M1 - pair, at + t * P:at + (t + 1) * P],
                                       shift[:, t * 512 + g * P:t * 512 + (g + 1) * P], ident_r[:, :],
                                       start=False, stop=(t == BT - 1), skip_group_check=True)
                mm.then_inc(qs_filled, 1)

            def scores_t(b, p, *us):
                for u in us:
                    pair, t, j = u // 8, u // 4 % 2, u % 4
                    pe.wait_ge(exp_done, TU * b + u + 1)
                    if u % 8 == 0:
                        pe.wait_ge(qs_ready, 2 * b + pair + 1)
                    first = isinstance(b, int) and b == 0
                    keep_clock(4 + u % 2, START_SCORES_T if first else int(u in CLOCK_UNITS))
                    r = slice(SLOT * j, SLOT * (j + 1))
                    for gg in range(2):
                        g = 2 * pair + gg
                        mm = pe.matmul(ps[:, 4 + u % 2, gg * SEQ:(gg + 1) * SEQ],
                                       qk4[r, p, g, 1, t * P:(t + 1) * P], qs4[r, g, :], start=True, stop=True)
                    mm.then_inc(t_filled, 1)

            def weigh(b, p, pair, *parts):
                if 0 in parts:
                    pe.wait_ge(exp_done, TU * b + 8 * pair + 8 + 2)
                for part in parts:
                    gg, t = part // 2, part % 2
                    for j in range(4):
                        h = 4 * (2 * pair + gg) + j
                        mm = pe.matmul(ps[SLOT * j:SLOT * (j + 1), M0 + pair, gg * SEQ:(gg + 1) * SEQ],
                                       v4[:, p, t, h, :], prob[:, 8 * pair + 4 * t + j, gg * SEQ:(gg + 1) * SEQ],
                                       start=(t == 0), stop=(t == BT - 1))
                if 3 in parts:
                    mm.then_inc(pv_filled, 1)

            def turn_y(b, t):
                pe.wait_ge(y4_ready, 2 * b + 2)
                for g in range(HG):
                    mm = pe.transpose(ps[:, M1 - t, g * P:(g + 1) * P], y4[:, g, t * P:(t + 1) * P], ident[:, :])
                mm.then_inc(yq_filled, 1)

            def transpose_y(b):
                pe.wait_ge(y_ready, 2 * b + 2)
                for t in range(BT):
                    mm = pe.transpose(ps[:, M1, t * P:(t + 1) * P], y_tok[:, t, :], ident[:, :])
                mm.then_inc(yt_filled, 1)

            def project_out(b):
                pe.wait_ge(yt_ready, b + 1)
                for t in range(BT):
                    rows = slice(t * P, (t + 1) * P)
                    mm = pass3(ps[:, M1, rows], yt_hi[:, rows], yt_lo[:, rows], wa_hi[:, 5, :], wa_lo[:, 5, :])
                mm.then_inc(o_filled, 1)

            def batch(b, p, tail=True, place_next=True, project_next=True):
                q, last = 1 - p, not place_next
                if place_next:
                    if tail:
                        pe.wait_ge(att_done, b)
                    pe.wait_ge(qs_ready, 2 * b + 1)
                    place(b + 1, q, 0)
                if tail:
                    pe.wait_ge(y4_ready, 2 * b - 1)
                else:
                    pe.wait_ge(v_ready, 1)
                if place_next:
                    place(b + 1, q, 1)
                scores_t(b, p, 0, 1)
                if place_next:
                    scores(b + 1, q, 0)
                    place(b + 1, q, 2)
                place_shifted(b, p, 1)
                scores_t(b, p, 2)
                if place_next:
                    scores(b + 1, q, 1)
                    pe.wait_ge(qs_ready, 2 * b + 2)
                    place(b + 1, q, 3)
                scores_t(b, p, 3)
                if place_next:
                    pe.wait_ge(qk4_ready, 4 * b + 7)
                else:
                    pe.wait_ge(att_done, b)
                if project_next:
                    a_transpose_x(b + 2)
                scores_t(b, p, 4)
                if place_next:
                    scores(b + 1, q, 2)
                    pe.wait_ge(qk4_ready, 4 * b + 8)
                scores_t(b, p, 5)
                if project_next:
                    qk(b + 2, p)
                if tail:
                    weigh(b - 1, q, 1, 0)
                scores_t(b, p, 6)
                if tail:
                    weigh(b - 1, q, 1, 1)
                if place_next:
                    scores(b + 1, q, 3)
                scores_t(b, p, 7)
                if project_next:
                    qk_swapped(b + 2, p)
                if tail:
                    weigh(b - 1, q, 1, 2)
                if place_next:
                    scores(b + 1, q, 4)
                if tail:
                    weigh(b - 1, q, 1, 3)
                scores_t(b, p, 8)
                if tail:
                    turn_y(b - 1, 0)
                if last:
                    transpose_x(GROUPS, 2)
                scores_t(b, p, 9)
                if project_next:
                    pe.wait_ge(sin_done, b + 3)
                if place_next:
                    values(b + 1, q)
                    scores(b + 1, q, 5)
                scores_t(b, p, 10)
                if place_next:
                    pe.wait_ge(v_ready, b + 2)
                if tail:
                    turn_y(b - 1, 1)
                if place_next:
                    scores(b + 1, q, 6)
                    if tail:
                        pe.wait_ge(y_ready, 2 * b - 1)
                    place_shifted(b + 1, q, 0)
                scores_t(b, p, 11)
                if place_next:
                    pe.wait_ge(qs_ready, 2 * b + 3)
                if tail:
                    transpose_y(b - 1)
                if last:
                    router(GROUPS, 3)
                weigh(b, p, 0, 0)
                if place_next:
                    scores(b + 1, q, 7)
                scores_t(b, p, 12)
                weigh(b, p, 0, 1)
                if tail:
                    project_out(b - 1)
                scores_t(b, p, 13)
                weigh(b, p, 0, 2, 3)
                scores_t(b, p, 14, 15)
                if last:
                    transpose_gates(GROUPS, 3)

            def attention():
                place(0, 0, 0)
                qk_swapped(1, 1)
                pe.wait_ge(sin_done, 2)
                place(0, 0, 1)
                transpose_out(GROUPS - 1, 3)
                pe.wait_ge(qk4_ready, 1)
                place(0, 0, 2)
                scores(0, 0, 0)
                pe.wait_ge(qk4_ready, 2)
                place(0, 0, 3)
                pe.wait_ge(post_ready, GROUPS)
                scores(0, 0, 1)
                pe.wait_ge(ones_set, 1)
                pe.wait_ge(qk4_ready, 4)
                values(0, 0)
                scores(0, 0, 2, 3, 4)
                pe.wait_ge(shift_zeroed, 1)
                place_shifted(0, 0, 0)
                scores(0, 0, 5, 6, 7)
                batch(0, 0, tail=False)
                with pe.Fori(0, 2) as i:
                    batch(2 * i + 1, 1)
                    batch(2 * i + 2, 0)
                batch(5, 1)
                batch(6, 0, project_next=False)
                batch(7, 1, place_next=False, project_next=False)
                pe.wait_ge(att_done, BATCH)
                weigh(BATCH - 1, 1, 1, 0, 1, 2, 3)
                turn_y(BATCH - 1, 0)
                turn_y(BATCH - 1, 1)
                transpose_y(BATCH - 1)
                project_out(BATCH - 1)

            pe.wait_ge(eye_loaded, 16)
            pe.wait_ge(eye_split, 1)
            first_head()
            body(0, 0, first=True)
            with pe.Fori(1, GROUPS - 1) as g:
                body(0, g)
            body(0, GROUPS - 1, last=True)

            attention()

            second_head()
            body(1, 0)
            with pe.Fori(1, GROUPS - 1) as g:
                body(1, g)
            body(1, GROUPS - 1, last=True)

        @block.scalar
        def _(act):
            def copy_x(n, g, bank=M0):
                act.wait_ge(xt_filled, n + 1)
                act.activation(x_t[:, :], ps[:, bank, :], ACT.Copy)
                act.activation(x_hi[:, bass.ds(g * GROUP, GROUP)], ps[:, bank, :], ACT.Copy).then_inc(xt_copied, 1)

            def copy_gates(n, bank=M1):
                act.wait_ge(gt_filled, n + 1)
                if not (isinstance(n, int) and n == 0):
                    act.wait_ge(gt_stored, 16 * n)
                act.activation(gates_t[:, :], ps[0:EXPERTS, bank, :], ACT.Copy).then_inc(gt_copied, 1)

            def gelu(n, e):
                s = n * EXPERTS + e
                if not (isinstance(s, int) and s < 2):
                    act.wait_ge(down_filled, s - 1)
                for c in range(CH):
                    act.wait_ge(up_filled, s * CH + c + 1)
                    act.activation(g_hi[:, e % 2, c, :], ps[:, c, :], ACT.Gelu, bias=b1_sb[:, e, c:c + 1])
                    if not (isinstance(s, int) and s == 0):
                        act.wait_ge(lo_done, (s - 1) * CH + c + 1)
                    act.activation(g_full[:, c, :], ps[:, c, :], ACT.Gelu, bias=b1_sb[:, e, c:c + 1])\
                        .then_inc(gelu_done, 1)

            def a_copy_x(b, p):
                act.wait_ge(a_xt_filled, b + 1)
                act.activation(ax_hi[:, p, :], ps[:, M1, 0:SEQ], ACT.Copy).then_inc(a_xhi_done, 1)

            def body(phase, g, last=False):
                n = phase * GROUPS + g
                for e in range(EXPERTS):
                    if e + 2 < EXPERTS:
                        gelu(n, e + 2)
                    elif not last:
                        gelu(n + 1, e + 2 - EXPERTS)
                    if not last:
                        if e == 3:
                            copy_x(n + 1, g + 1)
                        if e == 6:
                            copy_gates(n + 1)
                    elif phase == 0 and e in (3, 5):
                        a_copy_x(e // 2 - 1, e // 2 - 1)

            def copy_values(b, p):
                act.wait_ge(v_filled, b + 1)
                act.activation(v4[:, p, :, :, 0:HD],
                               ps[:, M0, 0:SEQ].rearrange("p (t h c) -> p t h c", t=BT, h=HEADS),
                               ACT.Copy).then_inc(v_ready, 1)

            def copy_placed(b, p, g):
                act.wait_ge(sel_filled, 4 * b + g + 1)
                act.activation(qk4[:, p, g, :, :], ps[:, M1 - g % 2, :].rearrange("p (m n) -> p m n", m=2),
                               ACT.Identity, bias=shift_row[:, :]).then_inc(qk4_ready, 1)

            def copy_shifted(b, pair):
                act.wait_ge(qs_filled, 2 * b + pair + 1)
                act.activation(qs4[:, 2 * pair:2 * pair + 2, :],
                               ps[:, M1 - pair, :].rearrange("p (g n) -> p g n", g=2), ACT.Copy).then_inc(qs_ready, 1)

            def exps(b, *us):
                for u in us:
                    act.wait_ge(t_filled, TU * b + u + 1)
                    act.activation(prob[:, u, :], ps[:, 4 + u % 2, :], ACT.Exp, scale=SCALE).then_inc(exp_done, 1)

            def copy_weighed(b, pair):
                act.wait_ge(pv_filled, 2 * b + pair + 1)
                act.activation(y4[:, 2 * pair:2 * pair + 2, :],
                               ps[:, M0 + pair, :].rearrange("p (g n) -> p g n", g=2), ACT.Copy).then_inc(y4_ready, 1)

            def copy_y(b):
                act.wait_ge(yt_filled, b + 1)
                act.activation(yt_hi, ps[:, M1, 0:SEQ], ACT.Copy).then_inc(ythi_done, 1)

            def batch(b, p, tail=True, place_next=True, project_next=True):
                q, last = 1 - p, not place_next
                if place_next:
                    copy_placed(b + 1, q, 0)
                    copy_placed(b + 1, q, 1)
                exps(b, 0, 1)
                if place_next:
                    copy_placed(b + 1, q, 2)
                copy_shifted(b, 1)
                exps(b, 2)
                if place_next:
                    copy_placed(b + 1, q, 3)
                exps(b, 3)
                if project_next:
                    a_copy_x(b + 2, p)
                exps(b, 4, 5, 6, 7)
                if tail:
                    copy_weighed(b - 1, 1)
                exps(b, 8)
                if last:
                    copy_x(GROUPS, 0, 2)
                exps(b, 9)
                if place_next:
                    copy_values(b + 1, q)
                exps(b, 10)
                if place_next:
                    copy_shifted(b + 1, 0)
                exps(b, 11)
                if tail:
                    copy_y(b - 1)
                exps(b, 12, 13)
                copy_weighed(b, 0)
                exps(b, 14, 15)
                if last:
                    copy_gates(GROUPS, 3)

            def attention():
                copy_placed(0, 0, 0)
                copy_placed(0, 0, 1)
                copy_placed(0, 0, 2)
                copy_placed(0, 0, 3)
                act.wait_ge(ones_set, 1)
                copy_values(0, 0)
                copy_shifted(0, 0)
                batch(0, 0, tail=False)
                with act.Fori(0, 2) as i:
                    batch(2 * i + 1, 1)
                    batch(2 * i + 2, 0)
                batch(5, 1)
                batch(6, 0, project_next=False)
                batch(7, 1, place_next=False, project_next=False)
                copy_weighed(BATCH - 1, 1)
                copy_y(BATCH - 1)

            act.wait_ge(consts_set, 3)
            act.activation(rden[:, 0:GT], neg_half, ACT.Gelu)
            act.wait_ge(small_loaded, 16 * SMALL)
            copy_x(0, 0)
            gelu(0, 0)
            copy_gates(0)
            gelu(0, 1)
            with act.Fori(0, GROUPS - 1) as g:
                body(0, g)
            body(0, GROUPS - 1, last=True)

            act.sem_inc(exp_done, 2)
            act.wait_ge(att_split, 3)
            attention()

            gelu(GROUPS, 0)
            gelu(GROUPS, 1)
            body(1, 0)
            with act.Fori(1, GROUPS - 1) as g:
                body(1, g)
            body(1, GROUPS - 1, last=True)

        @block.vector
        def _(vec):
            def norm_stats(src, count, norm, i):
                stats_done, var_ready, _ = norm
                for t in range(count):
                    vec.bn_stats(stats[:, t, :], src(t)).then_inc(stats_done, 1)
                vec.wait_ge(stats_done, (i + 1) * count)
                vec.memset(pad, 0.0)
                for t in range(count):
                    aggr = vec.bn_aggr(mv[:, t, :], stats[:, t, :])
                aggr.then_inc(var_ready, 1)

            def norm_apply(dst, src, count, norm, i):
                _, var_ready, rstd_ready = norm
                vec.wait_ge(var_ready, i + 1)
                vec.wait_ge(rstd_ready, 2 * i + 2)
                for t in range(count):
                    last = vec.tensor_scalar(dst(t), src(t), mv[:, t, 0:1], rstd[:, t:t + 1],
                                             ALU.subtract, ALU.mult)
                return last

            def x_tile(g, t, n):
                return x_tok[:, bass.ds(g * n + t, 1), :].rearrange("p a d -> p (a d)")

            def norm_in(g, n, stats_part=True, apply_part=True):
                if stats_part:
                    norm_stats(lambda t: x_tile(g, t, GT), GT, pre_norm, n)
                if apply_part:
                    norm_apply(lambda t: xn[:, t, :], lambda t: x_tile(g, t, GT), GT, pre_norm, n)\
                        .then_inc(ln_done, 1)

            def low_x(n, g, bank=M0):
                vec.wait_ge(xt_copied, n + 1)
                cols = bass.ds(g * GROUP, GROUP)
                vec.tensor_tensor(x_lo[:, cols], ps[:, bank, :], x_hi[:, cols].bitcast(F32),
                                  ALU.subtract).then_inc(xlo_done, 1)

            def gating(n, first_part=True, second_part=True, bank=M1):
                iota_b = iota_sb[:, :].unsqueeze(1).broadcast_to([P, GT, EXPERTS])
                if first_part:
                    at = Steps(n * GATE_STEPS)
                    vec.wait_ge(logits_filled, n + 1)
                    vec.tensor_tensor(logits[:, :, :], ps[:, bank, 0:GT * EXPERTS].rearrange("p (t e) -> p t e", t=GT),
                                      bg_sb[:, :].unsqueeze(1).broadcast_to([P, GT, EXPERTS]),
                                      ALU.add).then_inc(gate_steps, at.up())
                    vec.wait_ge(gate_steps, at.now())
                    vec.memset(pad, 0.0)
                    for t in range(GT):
                        op = vec.max(top[:, t, :], logits[:, t, :])
                    op.then_inc(gate_steps, at.up())
                    vec.wait_ge(gate_steps, at.now())
                    vec.tensor_tensor(gap, top[:, :, 1], top[:, :, 0], ALU.subtract).then_inc(gap_ready, 1)
                    for t in range(GT):
                        op = vec.max_index(top_at[:, t, :], top[:, t, :], logits[:, t, :])
                    op.then_inc(gate_steps, at.up())
                    vec.wait_ge(gate_steps, at.now())
                    vec.tensor_copy(top_f[:, :, :], top_at[:, :, 0:2]).then_inc(gate_steps, at.up())
                    vec.wait_ge(gate_steps, at.now())
                    vec.tensor_tensor(pick1[:, :, :], iota_b, top_f[:, :, 0:1].broadcast_to([P, GT, EXPERTS]),
                                      ALU.is_equal)
                    vec.tensor_tensor(gates[:, :, :], iota_b, top_f[:, :, 1:2].broadcast_to([P, GT, EXPERTS]),
                                      ALU.is_equal)
                if second_part:
                    at = Steps(n * GATE_STEPS + 4)
                    vec.wait_ge(e2_ready, n + 1)
                    vec.tensor_scalar(share2[:, :], e2, 1.0, None, ALU.add).then_inc(gate_steps, at.up())
                    vec.wait_ge(gate_steps, at.now())
                    vec.reciprocal(share1, share2[:, :]).then_inc(gate_steps, at.up())
                    vec.wait_ge(gate_steps, at.now())
                    vec.tensor_tensor(share2[:, :], e2, share1, ALU.mult).then_inc(gate_steps, at.up())
                    vec.tensor_tensor(pick1[:, :, :], pick1[:, :, :],
                                      share1.unsqueeze(2).broadcast_to([P, GT, EXPERTS]), ALU.mult)
                    vec.wait_ge(gate_steps, at.now())
                    vec.tensor_tensor(gates[:, :, :], gates[:, :, :],
                                      share2[:, :].unsqueeze(2).broadcast_to([P, GT, EXPERTS]),
                                      ALU.mult).then_inc(gate_steps, at.up())
                    vec.wait_ge(gate_steps, at.now())
                    vec.tensor_tensor(gates[:, :, :], gates[:, :, :], pick1[:, :, :], ALU.add).then_inc(gates_ready, 1)
                    assert 4 + at.n == GATE_STEPS

            def scale_out(n, e):
                s = n * EXPERTS + e
                vec.wait_ge(down_filled, s + 1)
                vec.wait_ge(gate_b_loaded[e], 16 * n + 16)
                if not (isinstance(s, int) and s < 2):
                    vec.wait_ge(acc_done, s - 1)
                vec.tensor_tensor(tmp[:, e % 2, :], ps[:, 4 + e % 2, :], gate_b[:, e, :],
                                  ALU.mult).then_inc(scaled, 1)
                if e == 0:
                    vec.wait_ge(scaled, s + 1)
                    vec.wait_ge(base_filled, n + 1)
                    if not (isinstance(n, int) and n == 0):
                        vec.wait_ge(tail_filled, n)
                    vec.tensor_tensor(acc[:, :], ps[:, M0, :], tmp[:, 0, :], ALU.add).then_inc(acc_done, 1)

            def low_g(n, e):
                s = n * EXPERTS + e
                for c in range(CH):
                    vec.wait_ge(gelu_done, s * CH + c + 1)
                    vec.tensor_tensor(g_lo[:, e % 2, c, :], g_full[:, c, :], g_hi[:, e % 2, c, :].bitcast(F32),
                                      ALU.subtract).then_inc(lo_done, 1)

            def finish(g, n, stats_part=True, apply_part=True, bank=M1):
                if stats_part:
                    vec.wait_ge(tail_filled, n + 1)
                    norm_stats(lambda t: ps[:, bank, t * P:(t + 1) * P], GT, post_norm, n)
                if apply_part:
                    norm_apply(lambda t: post[:, t, :], lambda t: ps[:, bank, t * P:(t + 1) * P],
                               GT, post_norm, n).then_inc(post_ready, 1)
                    vec.wait_ge(post_ready, n + 1)
                    vec.tensor_tensor(post[:, :, :], post[:, :, :], gam[:, :].unsqueeze(1).broadcast_to([P, GT, D]),
                                      ALU.mult).then_inc(scaled_post, 1)
                    vec.wait_ge(scaled_post, n + 1)
                    vec.wait_ge(beta_added, n + 1)
                    vec.tensor_tensor(x_tok[:, tiles(g), :], x_tok[:, tiles(g), :], post[:, :, :],
                                      ALU.add).then_inc(x_done, 1)

            def split_high(e):
                vec.wait_ge(w_loaded[e], 32)
                vec.tensor_copy(w_hi[:, :, e, :], w_raw[:, :, e, :]).then_inc(w_hi_done, 1)

            def a_norm(b, stats_part=True, apply_part=True):
                if stats_part:
                    norm_stats(lambda t: x_tile(b, t, BT), BT, att_norm, b)
                if apply_part:
                    norm_apply(lambda t: xn[:, t, :], lambda t: x_tile(b, t, BT), BT, att_norm, b)\
                        .then_inc(a_ln_done, 1)

            def a_low_x(b, p):
                vec.wait_ge(a_xhi_done, b + 1)
                vec.tensor_tensor(ax_lo[:, p, :], ps[:, M1, 0:SEQ], ax_hi[:, p, :].bitcast(F32),
                                  ALU.subtract).then_inc(a_xlo_done, 1)

            def rotate_cos(b):
                vec.wait_ge(qk_filled, b + 1)
                vec.tensor_tensor(t_cos, ps[:, M0, :].rearrange("p (m n) -> p m n", m=2),
                                  rope_sb[:, 0:1, :].broadcast_to([P, 2, SEQ]), ALU.mult).then_inc(cos_done, 1)

            def rotate_sin(b, p):
                vec.wait_ge(qks_filled, b + 1)
                vec.tensor_tensor(t_sin, ps[:, M0, :].rearrange("p (m n) -> p m n", m=2),
                                  rope_sb[:, 1:2, :].broadcast_to([P, 2, SEQ]), ALU.mult).then_inc(sin_done, 1)
                vec.wait_ge(sin_done, b + 1)
                if not (isinstance(b, int) and b == 0):
                    vec.wait_ge(rot_ready, b)
                vec.tensor_tensor(rot, t_cos, t_sin, ALU.add).then_inc(rot_sum, 1)
                vec.wait_ge(rot_sum, b + 1)
                vec.tensor_copy(rot_hi[:, p, :, :], rot).then_inc(rot_hi_done, 1)

            def maxima(b, *us):
                for u in us:
                    pair, t, jp = u // 4, u // 2 % 2, u % 2
                    vec.wait_ge(s_filled, SU * b + u + 1)
                    vec.tensor_reduce(
                        mx[:, t, :].rearrange("p (r g j) -> p r j g", r=2, g=2)[:, pair, 2 * jp:2 * jp + 2, :],
                        ps[:, 2 * (u % 2):2 * (u % 2) + 2, :].rearrange("p j (g n) -> p j g n", g=2),
                        AX.X, ALU.max).then_inc(max_done, 1)

            def start_attention(e):
                if e == 0:
                    vec.wait_ge(att_loaded, 32)
                    vec.tensor_copy(sel_r[:, :, :, :].rearrange("p a g m -> p (a g m)"), sel_raw)\
                        .then_inc(att_split, 1)
                if e == 1:
                    vec.wait_ge(x_done, GROUPS - 1)
                    a_norm(0, apply_part=False)
                if e == 2:
                    a_norm(0, stats_part=False)
                    wa_flat = wa_hi[:, :, :].rearrange("p a m -> p (a m)")
                    vec.tensor_copy(wa_flat, wa_raw).then_inc(att_split, 1)
                    vec.wait_ge(att_split, 2)
                    vec.tensor_tensor(wa_lo[:, :, :].rearrange("p a m -> p (a m)"), wa_raw,
                                      wa_flat.bitcast(F32), ALU.subtract).then_inc(att_split, 1)
                if e == 3:
                    a_norm(1, apply_part=False)
                if e == 4:
                    a_low_x(0, 0)
                    a_norm(1, stats_part=False)
                if e == 5:
                    rotate_cos(0)
                if e == 6:
                    rotate_sin(0, 0)
                    a_low_x(1, 1)
                if e == 7:
                    rotate_cos(1)

            def body(phase, g, first=False, last=False):
                n = phase * GROUPS + g
                for e in range(EXPERTS):
                    scale_out(n, e)
                    if e == 5 and not last:
                        gating(n + 1, second_part=False)
                    if e + 2 < EXPERTS:
                        low_g(n, e + 2)
                    elif not last:
                        low_g(n + 1, e + 2 - EXPERTS)
                    if first and e + 4 < EXPERTS:
                        split_high(e + 4)
                    behind = not (isinstance(g, int) and g == 0)
                    if e == 0 and behind:
                        finish(g - 1, n - 1, apply_part=False)
                    if e == 1 and behind:
                        finish(g - 1, n - 1, stats_part=False)
                    if not last:
                        if e == 1:
                            if first:
                                for later in x_loaded[1:]:
                                    vec.wait_ge(later, 16)
                            norm_in(g + 1, n + 1, apply_part=False)
                        if e == 2:
                            norm_in(g + 1, n + 1, stats_part=False)
                        if e == 4:
                            low_x(n + 1, g + 1)
                        if e == 5:
                            gating(n + 1, first_part=False)
                    elif phase == 0:
                        start_attention(e)
                if last and phase == 0:
                    rotate_sin(1, 1)
                    finish(g, n, apply_part=False, bank=3)
                    maxima(0, 0)
                    finish(g, n, stats_part=False, bank=3)
                elif last:
                    finish(g, n)

            def first_head():
                norm_in(0, 0)
                split_high(0)
                low_x(0, 0)
                split_high(1)
                split_high(2)
                vec.wait_ge(small_loaded, 16 * SMALL)
                gating(0)
                split_high(3)
                low_g(0, 0)
                low_g(0, 1)

            def negate(b, pair):
                vec.wait_ge(max_done, SU * b + 4 * pair + 4 + 2)
                vec.tensor_scalar(shift_v[:, :, 8 * pair:8 * pair + 8, 24:25].rearrange("p t h c -> p t (h c)"),
                                  mx[:, :, 8 * pair:8 * pair + 8], -1.0, None, ALU.mult).then_inc(shift_ready, 1)

            def divide(b, t):
                vec.wait_ge(yq_filled, 2 * b + t + 1)
                heads = ps[:, M1 - t, :].rearrange("p (h c) -> p h c", h=HEADS)
                if t == 1 or not (isinstance(b, int) and b == 0):
                    vec.wait_ge(y_ready, 2 * b + t)
                vec.reciprocal(rden[:, :], heads[:, :, HD]).then_inc(rden_ready, 1)
                vec.wait_ge(rden_ready, 2 * b + t + 1)
                vec.tensor_tensor(y_tok[:, t, :].rearrange("p (h c) -> p h c", h=HEADS), heads[:, :, 0:HD],
                                  rden[:, :].unsqueeze(2).broadcast_to([P, HEADS, HD]),
                                  ALU.mult).then_inc(y_ready, 1)

            def low_y(b):
                vec.wait_ge(ythi_done, b + 1)
                vec.tensor_tensor(yt_lo, ps[:, M1, 0:SEQ], yt_hi.bitcast(F32), ALU.subtract).then_inc(yt_ready, 1)

            def add_attention(b):
                vec.wait_ge(o_filled, b + 1)
                vec.tensor_tensor(x_tok[:, tiles(b, BT), :], ps[:, M1, 0:SEQ].rearrange("p (t d) -> p t d", t=BT),
                                  x_tok[:, tiles(b, BT), :], ALU.add).then_inc(att_done, 1)

            def batch(b, p, tail=True, place_next=True, project_next=True, norm=True):
                last = not place_next
                if place_next:
                    maxima(b + 1, 0, 1)
                if project_next:
                    a_low_x(b + 2, p)
                if place_next:
                    maxima(b + 1, 2)
                if project_next:
                    rotate_cos(b + 2)
                if place_next:
                    maxima(b + 1, 3)
                    negate(b + 1, 0)
                if project_next:
                    rotate_sin(b + 2, p)
                if place_next:
                    maxima(b + 1, 4)
                if norm:
                    a_norm(b + 3, apply_part=False)
                if last:
                    norm_in(0, GROUPS)
                if tail:
                    divide(b - 1, 0)
                if place_next:
                    maxima(b + 1, 5)
                if last:
                    low_x(GROUPS, 0, 2)
                if tail:
                    divide(b - 1, 1)
                if last:
                    gating(GROUPS, second_part=False, bank=3)
                if place_next:
                    maxima(b + 1, 6)
                if norm:
                    a_norm(b + 3, stats_part=False)
                if tail:
                    low_y(b - 1)
                if place_next:
                    maxima(b + 1, 7)
                    negate(b + 1, 1)
                if tail:
                    add_attention(b - 1)
                if last:
                    gating(GROUPS, first_part=False)

            def attention():
                maxima(0, 1)
                a_norm(2, apply_part=False)
                maxima(0, 2)
                a_norm(2, stats_part=False)
                maxima(0, 3)
                vec.wait_ge(shift_zeroed, 1)
                negate(0, 0)
                maxima(0, 4, 5, 6, 7)
                negate(0, 1)
                batch(0, 0, tail=False)
                with vec.Fori(0, 2) as i:
                    batch(2 * i + 1, 1)
                    batch(2 * i + 2, 0)
                batch(5, 1, norm=False)
                batch(6, 0, project_next=False, norm=False)
                batch(7, 1, place_next=False, project_next=False, norm=False)
                divide(BATCH - 1, 0)
                divide(BATCH - 1, 1)
                low_y(BATCH - 1)
                add_attention(BATCH - 1)

            vec.wait_ge(eye_loaded, 16)
            vec.tensor_copy(ident_r[:, :], ident[:, :]).then_inc(eye_split, 1)
            vec.wait_ge(x_loaded[0], 16)
            first_head()
            vec.sem_inc(max_done, 2)
            vec.sem_inc(att_done, 1)
            body(0, 0, first=True)
            with vec.Fori(1, GROUPS - 1) as g:
                body(0, g)
            body(0, GROUPS - 1, last=True)

            attention()

            low_g(GROUPS, 0)
            low_g(GROUPS, 1)
            body(1, 0)
            with vec.Fori(1, GROUPS - 1) as g:
                body(1, g)
            body(1, GROUPS - 1, last=True)


def shape_constants():
    pair = np.arange(HD // 2, dtype=np.float32)
    angle = np.power(np.float32(10000.0), np.float32(2.0) * pair / np.float32(HD)).astype(np.float32)
    theta = (np.arange(SEQ, dtype=np.float32)[:, None] * angle[None, :]).astype(np.float32)
    cos, sin = np.cos(theta).astype(np.float32), np.sin(theta).astype(np.float32)
    rope = np.zeros((P, 2, SEQ), np.float32)
    for c in range(P):
        rope[c, 0] = cos[:, c % HD // 2]
        rope[c, 1] = sin[:, c % HD // 2] * (1 if c % 2 else -1)
    sel = np.zeros((P, 4, HG, P), np.float32)
    parts = ((0, 2), (1,), (0, 1), (2,))
    for kind, eights in enumerate(parts):
        for h in range(HEADS):
            g, j = h // 4, h % 4
            for r in eights:
                for c in range(HD):
                    sel[HD * h + c, kind, g, SLOT * j + HD * r + c] = 1.0
    ones_at = np.zeros((P, 1), np.float32)
    ones_at[24::SLOT] = 1.0
    iota8 = np.ascontiguousarray(np.broadcast_to(np.arange(EXPERTS, dtype=np.float32), (P, EXPERTS)))
    return dict(rope=rope, sel=sel.reshape(P, -1), ones_at=ones_at, eye=np.eye(P, dtype=np.float32), iota8=iota8)


def kernel(L0_attn_x, L0_attn_w_q, L0_attn_w_k, L0_attn_w_v, L0_attn_w_o, L0_ffn_Wg, L0_ffn_bg, L0_ffn_W1,
           L0_ffn_b1, L0_ffn_W2, L0_ffn_b2, L0_ffn_gamma, L0_ffn_beta):
    import concourse.bacc as bacc
    from concourse.bass_utils import run_bass_kernel_spmd

    def rows(a):
        a = np.asarray(a)
        return np.ascontiguousarray(np.broadcast_to(a, (P,) + a.shape))

    swap = np.arange(P).reshape(-1, 2)[:, ::-1].reshape(-1)
    wq, wk, wv, wo = (np.asarray(w) for w in (L0_attn_w_q, L0_attn_w_k, L0_attn_w_v, L0_attn_w_o))
    w1, w2 = np.asarray(L0_ffn_W1), np.asarray(L0_ffn_W2)
    arrays = dict(
        x=np.asarray(L0_attn_x).reshape(TILES, P, D),
        w1=w1.transpose(1, 0, 2),
        w2=w2.reshape(EXPERTS, CH, P, D).transpose(2, 0, 1, 3).reshape(P, EXPERTS, HID),
        wg=np.asarray(L0_ffn_Wg),
        bg=rows(L0_ffn_bg),
        b1=np.asarray(L0_ffn_b1).reshape(EXPERTS, CH, P).transpose(2, 0, 1),
        b2=np.asarray(L0_ffn_b2),
        gamma=rows(L0_ffn_gamma),
        beta=rows(L0_ffn_beta),
        watt=np.stack([wq.T, wk.T, wq[swap].T, wk[swap].T, wv.T, wo.T], axis=1).reshape(P, 6 * P),
        **shape_constants(),
    )
    arrays = {n: np.ascontiguousarray(a) for n, a in arrays.items()}
    nc = bacc.Bacc("TRN2", target_bir_lowering=False, num_devices=1)
    args = {n: nc.dram_tensor(n, a.shape, mybir.dt.from_np(a.dtype), kind="ExternalInput").ap()
            for n, a in arrays.items()}
    args["out"] = nc.dram_tensor("out", (TILES, P, D), F32, kind="ExternalOutput").ap()
    build(nc, **args)
    result = run_bass_kernel_spmd(nc, [arrays], core_ids=[0])
    return result.results[0]["out"].reshape(BATCH, SEQ, D)
```
